# Optimizing a Trainium2 kernel written in Bass

```python
import numpy as np
import jax
import jax.numpy as jnp

def _softmax(x, axis=-1):
    return jax.nn.softmax(x, axis=axis)

def _gelu(x):
    return jax.nn.gelu(x, approximate=True)

def _silu(x):
    return jax.nn.silu(x)

def _sigmoid(x):
    return jax.nn.sigmoid(x)

def _layernorm(x, axis=-1, eps=1e-05):
    m = jnp.mean(x, axis=axis, keepdims=True)
    v = jnp.var(x, axis=axis, keepdims=True)
    return (x - m) / jnp.sqrt(v + eps)

def _scatter_add(tgt, idx, src, axis=0):
    return tgt.at[idx].add(src)

def _segment_sum(src, seg, n):
    return jax.ops.segment_sum(src, seg, n)
kernel_name = 'mk_cond_resid_d2_seqx_r8_b22b8f'

def setup_inputs(seed: int=0):
    np.random.seed(seed)
    _w = jnp.asarray

    def _rec_inputs():
        import jax
        import jax.numpy as jnp
        _rk = jax.random.key(seed)
        x = -0.0003929 + 0.9999 * jax.random.normal(jax.random.fold_in(_rk, 1), (32, 128, 128), jnp.float32)
        _lenS = 128 - jax.random.randint(jax.random.fold_in(_rk, 7), (32,), 0, max(1, 128 // 4) + 1, jnp.int32)
        _lenS2 = 128 - jax.random.randint(jax.random.fold_in(_rk, 8), (32,), 0, max(1, 128 // 4) + 1, jnp.int32)
        fside_Bx1x1024x16_0 = 0.00222621 + 0.99962 * jax.random.normal(jax.random.fold_in(_rk, 11), (32, 1, 128, 16), jnp.float32)
        cond_1024 = -0.00745576 + 0.997402 * jax.random.normal(jax.random.fold_in(_rk, 12), (32, 128), jnp.float32)
        return (x, fside_Bx1x1024x16_0, cond_1024)
    x, fside_Bx1x1024x16_0, cond_1024 = _rec_inputs()

    def _L0_cond_setup():
        import jax, jax.numpy as jnp
        import numpy as np
        B, F_, IN, OUT, R = (32, 64, 128, 128, 16)
        key = jax.random.key(seed)
        ks = jax.random.split(key, 6)
        x = jax.random.normal(ks[0], (B, F_, IN), dtype=jnp.float32)
        u = jax.random.normal(ks[1], (B, 1, OUT, R), dtype=jnp.float32)
        v = jax.random.normal(ks[2], (B, 1, IN, R), dtype=jnp.float32)
        b = jax.random.normal(ks[3], (B, 1, OUT), dtype=jnp.float32)
        lim = 1.0 / np.sqrt(IN)
        W = jax.random.uniform(ks[4], (OUT, IN), minval=-lim, maxval=lim, dtype=jnp.float32)
        fc_bias = jax.random.uniform(ks[5], (OUT,), minval=-lim, maxval=lim, dtype=jnp.float32)
        return {'x': x, 'u': u, 'v': v, 'b': b, 'W': W, 'fc_bias': fc_bias}
    _L0_cond_all = _L0_cond_setup()
    _L0_cond_in = {k: v for k, v in _L0_cond_all.items() if k in ('W', 'fc_bias')}
    del _L0_cond_all

    def _L1_cond_setup():
        import jax, jax.numpy as jnp
        import numpy as np
        NUM_EXPERTS = 4
        TOP_K = 2
        key = jax.random.key(seed)
        ks = jax.random.split(key, 16)
        B, L, D, E, H = (8, 96, 128, NUM_EXPERTS, 512)
        s = 0.02
        return {'context_c': jax.random.normal(ks[0], (B, L, D), jnp.float32), 'time_cond': jax.random.normal(ks[1], (B, D), jnp.float32), 'gate_w': jax.random.normal(ks[2], (3 * D, E), jnp.float32) * s, 'gate_b': jnp.zeros((E,), jnp.float32), 'time_w': jax.random.normal(ks[3], (D, 2 * E), jnp.float32) * s, 'time_b': jnp.zeros((2 * E,), jnp.float32), 'ew1': jax.random.normal(ks[4], (E, D, H), jnp.float32) * s, 'eb1': jnp.zeros((E, H), jnp.float32), 'ew2': jax.random.normal(ks[5], (E, H, D), jnp.float32) * s, 'eb2': jnp.zeros((E, D), jnp.float32), 'sw1': jax.random.normal(ks[6], (D, H), jnp.float32) * s, 'sb1': jnp.zeros((H,), jnp.float32), 'sw2': jax.random.normal(ks[7], (H, D), jnp.float32) * s, 'sb2': jnp.zeros((D,), jnp.float32)}
    _L1_cond_all = _L1_cond_setup()
    _L1_cond_in = {k: v for k, v in _L1_cond_all.items() if k in ('gate_w', 'gate_b', 'time_w', 'time_b', 'ew1', 'eb1', 'ew2', 'eb2', 'sw1', 'sb1', 'sw2', 'sb2')}
    del _L1_cond_all
    return {'x': x, 'fside_Bx1x1024x16_0': fside_Bx1x1024x16_0, 'cond_1024': cond_1024, 'L0_cond_W': _L0_cond_in['W'], 'L0_cond_fc_bias': _L0_cond_in['fc_bias'], 'L1_cond_gate_w': _L1_cond_in['gate_w'], 'L1_cond_gate_b': _L1_cond_in['gate_b'], 'L1_cond_time_w': _L1_cond_in['time_w'], 'L1_cond_time_b': _L1_cond_in['time_b'], 'L1_cond_ew1': _L1_cond_in['ew1'], 'L1_cond_eb1': _L1_cond_in['eb1'], 'L1_cond_ew2': _L1_cond_in['ew2'], 'L1_cond_eb2': _L1_cond_in['eb2'], 'L1_cond_sw1': _L1_cond_in['sw1'], 'L1_cond_sb1': _L1_cond_in['sb1'], 'L1_cond_sw2': _L1_cond_in['sw2'], 'L1_cond_sb2': _L1_cond_in['sb2']}

def reference(x, fside_Bx1x1024x16_0, cond_1024, L0_cond_W, L0_cond_fc_bias, L1_cond_gate_w, L1_cond_gate_b, L1_cond_time_w, L1_cond_time_b, L1_cond_ew1, L1_cond_eb1, L1_cond_ew2, L1_cond_eb2, L1_cond_sw1, L1_cond_sb1, L1_cond_sw2, L1_cond_sb2):
    import jax
    import jax.numpy as jnp

    def _L0_cond_ref(x, u, v, b, W, fc_bias):
        import jax, jax.numpy as jnp
        import numpy as np
        B, F_, IN, OUT, R = (32, 64, 128, 128, 16)
        inch = x.shape[-1]
        r = v.shape[-1]
        z1 = jnp.einsum('bfi,bir->bfr', x, v[:, 0]) / inch
        z = jnp.einsum('bfr,bor->bfo', z1, u[:, 0]) / r
        y = jnp.einsum('bfi,oi->bfo', x, W) + fc_bias + z + b
        return jax.nn.gelu(y, approximate=False)

    def _L1_cond_ref(context_c, time_cond, gate_w, gate_b, time_w, time_b, ew1, eb1, ew2, eb2, sw1, sb1, sw2, sb2):
        import jax, jax.numpy as jnp
        import numpy as np
        NUM_EXPERTS = 4
        TOP_K = 2
        B, L, D = context_c.shape
        E, K = (NUM_EXPERTS, TOP_K)
        L_head = L_wrist = L // 3
        head = context_c[:, :L_head]
        wrist = context_c[:, L_head:L_head + L_wrist]
        proprio = context_c[:, L_head + L_wrist:]
        full_agg = context_c.mean(axis=1)
        hp_agg = jnp.concatenate([head, proprio], axis=1).mean(axis=1)
        wp_agg = jnp.concatenate([wrist, proprio], axis=1).mean(axis=1)
        gate_in = jnp.concatenate([full_agg, hp_agg, wp_agg], axis=-1)
        gate_logits = gate_in @ gate_w + gate_b
        mod = jax.nn.silu(time_cond) @ time_w + time_b
        scale, shift = jnp.split(mod, 2, axis=-1)
        gate_logits = gate_logits * (1.0 + scale) + shift
        gate_scores = jax.nn.softmax(gate_logits, axis=-1)
        topk_w, topk_i = jax.lax.top_k(gate_scores, K)
        topk_w = topk_w / (topk_w.sum(axis=-1, keepdims=True) + 1e-08)
        onehot = (topk_i[..., None] == jnp.arange(E)[None, None, :]).astype(context_c.dtype)
        w_be = jnp.sum(topk_w[..., None] * onehot, axis=1)
        mask = np.ones((E, L), dtype=np.float32)
        mask[1, L_head:L_head + L_wrist] = 0.0
        mask[2, :L_head] = 0.0
        mask = jnp.asarray(mask)
        out = jnp.zeros_like(context_c)
        for e in range(E):
            h = jax.nn.gelu(context_c @ ew1[e] + eb1[e], approximate=True)
            y = h @ ew2[e] + eb2[e]
            out = out + w_be[:, e][:, None, None] * mask[e][None, :, None] * y
        shared = jax.nn.gelu(context_c @ sw1 + sb1, approximate=True) @ sw2 + sb2
        return out + shared
    x = x + _L0_cond_ref(x, fside_Bx1x1024x16_0, fside_Bx1x1024x16_0, cond_1024[:, None, :], L0_cond_W, L0_cond_fc_bias)
    x = x + _L1_cond_ref(x, cond_1024, L1_cond_gate_w, L1_cond_gate_b, L1_cond_time_w, L1_cond_time_b, L1_cond_ew1, L1_cond_eb1, L1_cond_ew2, L1_cond_eb2, L1_cond_sw1, L1_cond_sb1, L1_cond_sw2, L1_cond_sb2)
    return x

_drawn_inputs = setup_inputs


def setup_inputs(seed=0):
    import zlib

    import numpy as np

    out = dict(_drawn_inputs(seed))
    spreads = {'L1_cond_gate_b': (0.0, 0.1),
     'L1_cond_time_b': (0.0, 0.275),
     'L1_cond_eb1': (0.0, 0.695),
     'L1_cond_eb2': (0.0, 0.1),
     'L1_cond_sb1': (0.0, 0.411),
     'L1_cond_sb2': (0.0, 0.1)}
    factors = {'fside_Bx1x1024x16_0': 4.721}
    for name, (base, spread) in spreads.items():
        noise = np.random.default_rng([zlib.crc32(name.encode()), seed]).standard_normal(out[name].shape)
        drawn = base * np.exp(spread * noise) if base else spread * noise
        out[name] = jnp.asarray(drawn.astype(out[name].dtype))
    for name, factor in factors.items():
        out[name] = (out[name] * factor).astype(out[name].dtype)
    return out
```

```python
from contextlib import ExitStack

import concourse.bass as bass
from concourse import mybir

F32 = mybir.dt.float32
F32R = mybir.dt.float32r
ALU = mybir.AluOpType
ACT = mybir.ActivationFunctionType
AX = mybir.AxisListType


def build(nc, x, fside, cond, W, fc_bias, gate_w, gate_b, time_w, time_b,
          ew1, eb1, ew2, eb2, sw1, sb1, sw2, sb2, out):
    B, L, D = x.shape
    R = fside.shape[-1]
    E, _, H = ew1.shape
    NB = 4
    NT = B // NB
    TOK = NB * L
    CH = H // 128
    HEAD = L // 3
    PROP = L - 2 * HEAD
    SEGS = [(0, 0, HEAD), (HEAD, 2 * HEAD, PROP), (HEAD + PROP, HEAD, HEAD)]
    NS = E + 1
    SPAN = [(0, L), (0, L), (0, HEAD + PROP), (HEAD, L), (0, L)]
    Z_SCALE = 1.0 / (D * R)
    ZR = NB * R
    KR = ZR + NB
    UP = 5
    BANK_Y, BANK_OUT, BANK_GATE = 5, 6, 7

    with ExitStack() as ctx:
        def sb(name, shape, dt=F32):
            return ctx.enter_context(nc.sbuf_tensor(name, shape, dt))

        def sem(name):
            return ctx.enter_context(nc.semaphore(name))

        ps = ctx.enter_context(nc.psum_tensor("ps", [128, 8, 512], F32))

        x_tok = sb("x_tok", [128, B, D])
        W_raw = sb("W_raw", [128, D])
        F_raw = sb("F_raw", [128, B * R])
        cond_raw = sb("cond_raw", [B, D])
        cond_rows = sb("cond_rows", [KR, NT, D])
        fcb = sb("fcb", [128, 1])
        sb2_col = sb("sb2_col", [128, 1])
        gate_raw = sb("gate_raw", [128, 3, E])
        gate_b_row = sb("gate_b_row", [B, E])
        time_w_raw = sb("time_w_raw", [128, 2 * E])
        time_b_row = sb("time_b_row", [B, 2 * E])
        eb2_raw = sb("eb2_raw", [E, D])
        b1_col = sb("b1_col", [128, NS, CH])
        W1_raw = sb("W1_raw", [128, 2, H])
        W2_raw = sb("W2_raw", [128, 2, H])
        ident = sb("ident", [128, 128])
        zmask = sb("zmask", [KR, NB, L])
        ones = sb("ones", [B, 128])
        before = sb("before", [B, E, E])
        own_batch = sb("own_batch", [B, B, E])
        seg_mask = sb("seg_mask", [E, 3])
        WT_hi = sb("WT_hi", [128, D], F32R)
        WT_lo = sb("WT_lo", [128, D], F32R)
        F_hi = sb("F_hi", [128, B * R], F32R)
        F_lo = sb("F_lo", [128, B * R], F32R)
        fT_hi = sb("fT_hi", [KR, NT, D], F32R)
        fT_lo = sb("fT_lo", [KR, NT, D], F32R)
        xT_hi = sb("xT_hi", [128, 2, TOK], F32R)
        xT_lo = sb("xT_lo", [128, 2, TOK], F32R)
        z1 = sb("z1", [ZR, 2, TOK])
        z1_hi = sb("z1_hi", [KR, 2, TOK], F32R)
        z1_lo = sb("z1_lo", [KR, 2, TOK], F32R)
        g0 = sb("g0", [128, 2, TOK])
        x1 = sb("x1", [128, NT * TOK])
        x1_hi = sb("x1_hi", [128, NT * TOK], F32R)
        x1_lo = sb("x1_lo", [128, NT * TOK], F32R)
        W1_hi = sb("W1_hi", [128, NS, CH, 128], F32R)
        W1_lo = sb("W1_lo", [128, NS, CH, 128], F32R)
        W2_hi = sb("W2_hi", [128, NS, CH, 128], F32R)
        W2_lo = sb("W2_lo", [128, NS, CH, 128], F32R)
        segsum = sb("segsum", [128, 3, B])
        gw = sb("gw", [128, 4, E])
        tw = sb("tw", [128, 2 * E])
        tanh_c = sb("tanh_c", [128, B])
        silu2 = sb("silu2", [128, B])
        gt = sb("gt", [B, 16, 2 * E])
        cmp_gt = sb("cmp_gt", [B, E, E])
        cmp_eq = sb("cmp_eq", [B, E, E])
        w_diag = sb("w_diag", [B, B, E])
        w_all = sb("w_all", [128, B * E])
        w_tile = sb("w_tile", [128, NB * E])
        wT = sb("wT", [E, B])
        wT_seg = sb("wT_seg", [E, 3, B])
        bias2 = sb("bias2", [128, 3, B])
        h = x_tok[:, :, :].rearrange("p b d -> p (b d)").rearrange("p (a c n) -> p a c n", a=2, c=CH)
        hs_hi = sb("hs_hi", [128, 2, CH, TOK], F32R)
        hs_lo = sb("hs_lo", [128, 2, CH, TOK], F32R)
        outT = sb("outT", [128, TOK])
        out_tok = sb("out_tok", [128, NB, D])

        x_in = [sem(f"x_in{p}") for p in range(NT // 2)]
        W_in, F_in, cond_in, cond_rows_in = sem("W_in"), sem("F_in"), sem("cond_in"), sem("cond_rows_in")
        fcb_in, small_in, b1_in = sem("fcb_in"), sem("small_in"), sem("b1_in")
        w1_in = [sem(f"w1_in{e}") for e in range(NS)]
        w2_in = [sem(f"w2_in{e}") for e in range(NS)]
        const_step, ident_ok, zmask_ok, gate_consts = (sem("const_step"), sem("ident_ok"), sem("zmask_ok"),
                                                       sem("gate_consts"))
        zbias_rows, fT_hi_ok, fT_lo_ok = sem("zbias_rows"), sem("fT_hi_ok"), sem("fT_lo_ok")
        WT_ps, fT_ps, condT_ps = sem("WT_ps"), sem("fT_ps"), sem("condT_ps")
        WT_hi_ok, WT_lo_ok, F_hi_ok, F_lo_ok = sem("WT_hi_ok"), sem("WT_lo_ok"), sem("F_hi_ok"), sem("F_lo_ok")
        w_hi_ok, w_lo_ok = sem("w_hi_ok"), sem("w_lo_ok")
        xT_ps, xT_hi_ok, xT_lo_ok = sem("xT_ps"), sem("xT_hi_ok"), sem("xT_lo_ok")
        z_ps, z1_ok, z1_hi_ok, z1_lo_ok = sem("z_ps"), sem("z1_ok"), sem("z1_hi_ok"), sem("z1_lo_ok")
        y0_ps, g0_ok, x1_ok, x1_hi_ok, x1_lo_ok = (sem("y0_ps"), sem("g0_ok"), sem("x1_ok"),
                                                   sem("x1_hi_ok"), sem("x1_lo_ok"))
        segsum_ok = sem("segsum_ok")
        tanh_c_ok, silu_ok, mod_ps, logit_ps = sem("tanh_c_ok"), sem("silu_ok"), sem("mod_ps"), sem("logit_ps")
        gate_step, mod_ok, gate_x, gate_tanh, w_ok = sem("gate_step"), sem("mod_ok"), sem("gate_x"), sem("gate_tanh"), sem("w_ok")
        w_bcast_ps, w_all_ok, wT_ok, bias_ps, bias_ok, x1b_ok = (
            sem("w_bcast_ps"), sem("w_all_ok"), sem("wT_ok"), sem("bias_ps"), sem("bias_ok"), sem("x1b_ok"))
        wT_seg_ok, w_tile_ok = sem("wT_seg_ok"), sem("w_tile_ok")
        up_ps, h_ok, hs_hi_ok, hs_lo_ok, down_ok = (sem("up_ps"), sem("h_ok"), sem("hs_hi_ok"),
                                                    sem("hs_lo_ok"), sem("down_ok"))
        outT_ok, out_ps, out_tok_ok, out_dma = sem("outT_ok"), sem("out_ps"), sem("out_tok_ok"), sem("out_dma")

        psA = [ps[:, 0, :], ps[:, 1, :]]
        psZ = [ps[0:ZR, 2, :], ps[0:ZR, 3, :]]
        psY0 = [ps[:, 4, :], ps[:, 5, :]]
        psY = ps[:, BANK_Y, :]
        psOut = ps[:, BANK_OUT, :]
        psWT = ps[:, BANK_GATE, 0:128]
        psFT = [ps[0:ZR, 6, :], ps[0:ZR, 5, :]]
        psCondT = ps[:, BANK_GATE, 128:128 + B]
        psMod = ps[0:B, BANK_GATE, 160:160 + 2 * E]
        psLogit = ps[0:B, BANK_GATE, 168:168 + E]
        psWgtT = ps[0:E, BANK_GATE, 176:176 + B]
        psBcast = ps[:, BANK_GATE, 256:256 + B * E]
        psBias = ps[:, BANK_GATE, 384:384 + 3 * B]

        block = ctx.enter_context(nc.Block())

        def f32(ap):
            return ap.bitcast(F32)

        def span(ap, s):
            a, z = SPAN[s]
            if (a, z) == (0, L):
                return ap
            return ap.rearrange("p (b l) -> p b l", l=L)[:, :, a:z]

        def half(par, s):
            return (NS * par + s) % 2

        def up_bank(s, c):
            a, z = SPAN[s]
            bank = ps[:, (s * CH + c) % UP, 0:NB * (z - a)]
            return bank if z - a == L else bank.rearrange("p (b l) -> p b l", b=NB)

        def weight(n):
            e = n // 2
            if n % 2 == 0:
                return (W1_raw[:, e % 2, :].rearrange("p (m c) -> p c m", c=CH), W1_hi[:, e, :, :], W1_lo[:, e, :, :])
            return (W2_raw[:, e % 2, :].rearrange("p (c m) -> p c m", c=CH), W2_hi[:, e, :, :], W2_lo[:, e, :, :])

        def load_weight(queue, n):
            e = n // 2
            if n % 2 == 0:
                queue.dma_start(W1_raw[:, e % 2, :], sw1 if e == 0 else ew1[e - 1]).then_inc(w1_in[e], 16)
            else:
                src = sw2 if e == 0 else ew2[e - 1]
                queue.dma_start(W2_raw[:, e % 2, :], src.rearrange("(p c) d -> p (c d)", c=CH)).then_inc(w2_in[e], 16)

        @block.sync
        def _(sp):
            def load_x(p):
                for at, src, n in SEGS:
                    b = 2 * NB * p
                    sp.dma_start(x_tok[at:at + n, b:b + 2 * NB, :],
                                 x[b:b + 2 * NB, src:src + n, :].rearrange("b l d -> l b d")).then_inc(x_in[p], 16)

            load_x(0)
            sp.dma_start(F_raw[:, :].rearrange("i (b r) -> i b r", r=R),
                         fside.rearrange("b a i r -> i (a b) r")).then_inc(F_in, 16)
            for p in range(1, NT // 2):
                load_x(p)
            for n in range(4, 2 * NS):
                sp.wait_ge(w_lo_ok, n - 3)
                load_weight(sp, n)
            with sp.Fori(0, NT, 1) as t:
                sp.wait_ge(out_tok_ok, t + 1)
                for at, dst, n in SEGS:
                    sp.dma_start(out[bass.ds(t * NB, NB), dst:dst + n, :].rearrange("b l d -> l b d"),
                                 out_tok[at:at + n, :, :]).then_inc(out_dma, 16)
            sp.wait_ge(out_dma, 16 * len(SEGS) * NT)

        @block.gpsimd
        def _(pool):
            n_const = 0

            def chained(ins):
                nonlocal n_const
                n_const += 1
                ins.then_inc(const_step, 1)
                pool.wait_ge(const_step, n_const)

            chained(nc.gpsimd.memset(ident[:, :], 0.0))
            nc.gpsimd.affine_select(out=ident[:, :], in_=ident[:, :], compare_op=ALU.not_equal, fill=1.0, base=0,
                                    pattern=[[-1, 128]], channel_multiplier=1).then_inc(ident_ok, 1)
            chained(nc.gpsimd.memset(zmask[:, :, :], Z_SCALE))
            chained(nc.gpsimd.affine_select(out=zmask[:, :, :], in_=zmask[:, :, :], compare_op=ALU.is_ge, fill=0.0,
                                            base=0, pattern=[[-R, NB], [0, L]], channel_multiplier=1))
            chained(nc.gpsimd.affine_select(out=zmask[:, :, :], in_=zmask[:, :, :], compare_op=ALU.is_ge, fill=0.0,
                                            base=R - 1, pattern=[[R, NB], [0, L]], channel_multiplier=-1))
            nc.gpsimd.affine_select(out=zmask[:, :, :], in_=zmask[:, :, :], compare_op=ALU.not_equal, fill=1.0,
                                    base=-ZR, pattern=[[-1, NB], [0, L]], channel_multiplier=1).then_inc(zmask_ok, 1)
            chained(nc.gpsimd.memset(before[:, :, :], 1.0))
            nc.gpsimd.affine_select(out=before[:, :, :], in_=before[:, :, :], compare_op=ALU.is_ge, fill=0.0,
                                    base=-1, pattern=[[1, E], [-1, E]], channel_multiplier=0).then_inc(gate_consts, 1)
            chained(nc.gpsimd.memset(own_batch[:, :, :], 0.0))
            nc.gpsimd.affine_select(out=own_batch[:, :, :], in_=own_batch[:, :, :], compare_op=ALU.not_equal,
                                    fill=1.0, base=0, pattern=[[-1, B], [0, E]],
                                    channel_multiplier=1).then_inc(gate_consts, 1)
            chained(nc.gpsimd.memset(seg_mask[:, :], 1.0))
            chained(nc.gpsimd.affine_select(out=seg_mask[:, 2:3], in_=seg_mask[:, 2:3], compare_op=ALU.not_equal,
                                            fill=0.0, base=-1, pattern=[[0, 1]], channel_multiplier=1))
            nc.gpsimd.affine_select(out=seg_mask[:, 0:1], in_=seg_mask[:, 0:1], compare_op=ALU.not_equal,
                                    fill=0.0, base=-2, pattern=[[0, 1]], channel_multiplier=1).then_inc(gate_consts, 1)
            nc.gpsimd.memset(ones[:, :], 1.0).then_inc(gate_consts, 1)

            def z1_low(t):
                pool.wait_ge(z1_hi_ok, t + 1)
                if t >= 2:
                    pool.wait_ge(y0_ps, t - 1)
                nc.gpsimd.tensor_tensor(z1_lo[0:ZR, t % 2, :], z1[:, t % 2, :], f32(z1_hi[0:ZR, t % 2, :]),
                                        ALU.subtract).then_inc(z1_lo_ok, 1)

            def x1_low(t):
                pool.wait_ge(x1_hi_ok, t + 1)
                c = slice(t * TOK, (t + 1) * TOK)
                nc.gpsimd.tensor_tensor(x1_lo[:, c], x1[:, c], f32(x1_hi[:, c]), ALU.subtract).then_inc(x1_lo_ok, 1)

            def weight_low(n):
                pool.wait_ge(w_hi_ok, n + 1)
                raw, hi, lo = weight(n)
                nc.gpsimd.tensor_tensor(lo, raw, f32(hi), ALU.subtract).then_inc(w_lo_ok, 1)

            for s in range(NT + 3):
                if 0 <= s - 1 < NT:
                    z1_low(s - 1)
                if 0 <= s - 3 < NT:
                    x1_low(s - 3)
                if s < 2 * NS:
                    weight_low(s)
            pool.wait_ge(bias_ok, 1)
            pool.wait_ge(x1_lo_ok, NT)
            pool.wait_ge(segsum_ok, 3 * NT)
            xb = x1[:, :].rearrange("p (b l) -> p b l", l=L)
            for i, (at, _, n) in enumerate(SEGS):
                nc.gpsimd.tensor_tensor(xb[:, :, at:at + n], xb[:, :, at:at + n],
                                        bias2[:, i, :].unsqueeze(2).to_broadcast([128, B, n]),
                                        ALU.add).then_inc(x1b_ok, 1)

        @block.scalar
        def _(act):
            act.dma_start(W_raw[:, :], W).then_inc(W_in, 16)
            act.dma_start(cond_rows[ZR:KR, :, :], cond.rearrange("(t j) d -> j t d", j=NB)).then_inc(cond_rows_in, 16)
            act.dma_start(fcb[:, :], fc_bias.rearrange("(p a) -> p a", a=1)).then_inc(fcb_in, 16)
            act.dma_start(cond_raw[:, :], cond).then_inc(cond_in, 16)
            for dst, src in (
                    (gate_raw[:, :, :], gate_w.rearrange("(g d) e -> d g e", g=3)),
                    (time_w_raw[:, :], time_w),
                    (gate_b_row[:, :], gate_b.rearrange("(a e) -> a e", a=1).to_broadcast([B, E])),
                    (time_b_row[:, :], time_b.rearrange("(a e) -> a e", a=1).to_broadcast([B, 2 * E])),
                    (eb2_raw[:, :], eb2),
                    (sb2_col[:, :], sb2.rearrange("(p a) -> p a", a=1))):
                act.dma_start(dst, src).then_inc(small_in, 16)
            act.dma_start(b1_col[:, 1:NS, :], eb1.rearrange("e (p c) -> p e c", c=CH)).then_inc(b1_in, 16)
            act.dma_start(b1_col[:, 0, :], sb1.rearrange("(p c) -> p c", c=CH)).then_inc(b1_in, 16)
            for n in range(4):
                load_weight(act, n)

            act.wait_ge(WT_ps, 1)
            nc.scalar.activation(WT_hi[:, :], psWT, ACT.Copy).then_inc(WT_hi_ok, 1)
            act.wait_ge(cond_rows_in, 16)
            nc.scalar.activation(fT_hi[ZR:KR, :, :], cond_rows[ZR:KR, :, :], ACT.Copy).then_inc(fT_hi_ok, 1)
            for i in range(2):
                act.wait_ge(fT_ps, i + 1)
                nc.scalar.activation(fT_hi[0:ZR, i * NT // 2:(i + 1) * NT // 2, :],
                                     psFT[i].rearrange("p (t d) -> p t d", d=D), ACT.Copy).then_inc(fT_hi_ok, 1)

            def xT_high(t):
                act.wait_ge(xT_ps, t + 1)
                if t >= 2:
                    act.wait_ge(y0_ps, t - 1)
                nc.scalar.activation(xT_hi[:, t % 2, :], psA[t % 2], ACT.Copy).then_inc(xT_hi_ok, 1)

            def z1_high(t):
                act.wait_ge(z1_ok, t + 1)
                if t >= 2:
                    act.wait_ge(y0_ps, t - 1)
                    act.wait_ge(z1_lo_ok, t - 1)
                nc.scalar.activation(z1_hi[0:ZR, t % 2, :], z1[:, t % 2, :], ACT.Copy).then_inc(z1_hi_ok, 1)

            def gelu0(t):
                act.wait_ge(y0_ps, t + 1)
                if t == 0:
                    act.wait_ge(fcb_in, 16)
                if t >= 2:
                    act.wait_ge(x1_ok, t - 1)
                nc.scalar.activation(g0[:, t % 2, :], psY0[t % 2], ACT.Gelu, bias=fcb[:, 0:1]).then_inc(g0_ok, 1)

            def x1_high(t):
                act.wait_ge(x1_ok, t + 1)
                c = slice(t * TOK, (t + 1) * TOK)
                nc.scalar.activation(x1_hi[:, c], x1[:, c], ACT.Copy).then_inc(x1_hi_ok, 1)

            def weight_high(n):
                act.wait_ge((w1_in if n % 2 == 0 else w2_in)[n // 2], 16)
                raw, hi, _ = weight(n)
                nc.scalar.activation(hi, raw, ACT.Copy).then_inc(w_hi_ok, 1)

            for s in range(NT + 3):
                if 0 <= s - 2 < NT:
                    gelu0(s - 2)
                if 0 <= s - 1 < NT:
                    z1_high(s - 1)
                if s < NT:
                    xT_high(s)
                if 0 <= s - 3 < NT:
                    x1_high(s - 3)
                if s < 2 * NS:
                    weight_high(s)
                if s == 3:
                    act.wait_ge(condT_ps, 1)
                    nc.scalar.activation(tanh_c[:, :], psCondT, ACT.Tanh, scale=0.5).then_inc(tanh_c_ok, 1)

            act.wait_ge(b1_in, 32)

            def gelu(t, par, s):
                k = NS * t + s
                if not isinstance(k, int) or k >= 2:
                    act.wait_ge(hs_lo_ok, CH * (k - 1))
                for c in range(CH):
                    act.wait_ge(up_ps, CH * k + c + 1)
                    nc.scalar.activation(span(h[:, half(par, s), c, :], s), up_bank(s, c), ACT.Gelu_apprx_tanh,
                                         bias=b1_col[:, s, c:c + 1]).then_inc(h_ok, 1)

            def tile(t, par, last=False):
                for s in range(2, NS):
                    gelu(t, par, s)
                if not last:
                    for s in range(2):
                        gelu(t + 1, 1 - par, s)
                act.wait_ge(out_ps, t + 1)
                act.wait_ge(out_dma, 16 * len(SEGS) * t)
                nc.scalar.activation(out_tok[:, :, :], psOut.rearrange("p (b d) -> p b d", d=D),
                                     ACT.Copy).then_inc(out_tok_ok, 1)

            gelu(0, 0, 0)
            act.wait_ge(gate_x, 1)
            nc.scalar.activation(gt[:, 4, 0:E], gt[:, 3, 0:E], ACT.Tanh, scale=0.5).then_inc(gate_tanh, 1)
            gelu(0, 0, 1)
            with act.Fori(0, NT - 2, 2) as t:
                tile(t, 0)
                tile(t + 1, 1)
            tile(NT - 2, 0)
            tile(NT - 1, 1, last=True)

        @block.tensor
        def _(pe):
            def product3(dst, w_hi, w_lo, m_hi, m_lo, start, stop):
                nc.tensor.matmul(dst, w_hi, m_hi, start=start, stop=False)
                nc.tensor.matmul(dst, w_hi, m_lo, start=False, stop=False)
                return nc.tensor.matmul(dst, w_lo, m_hi, start=False, stop=stop)

            def xT(t):
                pe.wait_ge(x_in[t // 2], 16 * len(SEGS))
                if t >= 2:
                    pe.wait_ge(x1_ok, t - 1)
                for b in range(NB):
                    last = nc.tensor.transpose(psA[t % 2][:, b * L:(b + 1) * L], x_tok[:, NB * t + b, :], ident[:, :])
                last.then_inc(xT_ps, 1)

            def low_rank_in(t):
                pe.wait_ge(xT_hi_ok, t + 1)
                pe.wait_ge(xT_lo_ok, t + 1)
                if t == 0:
                    pe.wait_ge(F_hi_ok, 1)
                    pe.wait_ge(F_lo_ok, 1)
                if t >= 2:
                    pe.wait_ge(z1_ok, t - 1)
                c = slice(t * ZR, (t + 1) * ZR)
                product3(psZ[t % 2], F_hi[:, c], F_lo[:, c], xT_hi[:, t % 2, :], xT_lo[:, t % 2, :],
                         True, True).then_inc(z_ps, 1)

            def layer0(t):
                if t == 0:
                    pe.wait_ge(WT_hi_ok, 1)
                    pe.wait_ge(WT_lo_ok, 1)
                    pe.wait_ge(fT_hi_ok, 3)
                    pe.wait_ge(fT_lo_ok, 3)
                    pe.wait_ge(zbias_rows, 4)
                if t >= 2:
                    pe.wait_ge(g0_ok, t - 1)
                product3(psY0[t % 2], WT_hi[:, :], WT_lo[:, :], xT_hi[:, t % 2, :], xT_lo[:, t % 2, :], True, False)
                pe.wait_ge(z1_hi_ok, t + 1)
                pe.wait_ge(z1_lo_ok, t + 1)
                product3(psY0[t % 2], fT_hi[:, t, :], fT_lo[:, t, :], z1_hi[:, t % 2, :], z1_lo[:, t % 2, :],
                         False, True).then_inc(y0_ps, 1)

            pe.wait_ge(ident_ok, 1)
            pe.wait_ge(W_in, 16)
            nc.tensor.transpose(psWT, W_raw[:, :], ident[:, :]).then_inc(WT_ps, 1)
            xT(0)
            pe.wait_ge(F_in, 16)
            for i in range(2):
                for j in range(NT // 2):
                    t = i * NT // 2 + j
                    last = nc.tensor.transpose(psFT[i][:, j * D:(j + 1) * D], F_raw[:, t * ZR:(t + 1) * ZR],
                                               ident[:, :])
                last.then_inc(fT_ps, 1)
            for s in range(1, NT + 2):
                if 0 <= s - 2 < NT:
                    layer0(s - 2)
                if 0 <= s - 1 < NT:
                    low_rank_in(s - 1)
                if s < NT:
                    xT(s)
                if s == 2:
                    pe.wait_ge(cond_in, 16)
                    nc.tensor.transpose(psCondT, cond_raw[:, :], ident[0:B, 0:B]).then_inc(condT_ps, 1)
                if s == NT:
                    pe.wait_ge(silu_ok, 1)
                    pe.wait_ge(gate_consts, 5)
                    nc.tensor.matmul(psMod, silu2[:, :], tw[:, :], start=True, stop=True).then_inc(mod_ps, 1)

            def up(t, par, s):
                k = NS * t + s
                if isinstance(t, int) and t == 0:
                    pe.wait_ge(w_lo_ok, 2 * s + 1)
                for c in range(CH):
                    n = CH * k + c
                    if not isinstance(n, int) or n >= UP:
                        pe.wait_ge(h_ok, n - UP + 1)
                    cols = bass.ds(t * TOK, TOK)
                    product3(up_bank(s, c), W1_hi[:, s, c, :], W1_lo[:, s, c, :],
                             span(x1_hi[:, cols], s), span(x1_lo[:, cols], s), True, True).then_inc(up_ps, 1)

            def down(t, par, s):
                k = NS * t + s
                if isinstance(t, int) and t == 0:
                    pe.wait_ge(w_lo_ok, 2 * s + 2)
                if s == 0:
                    pe.wait_ge(outT_ok, t)
                for c in range(CH):
                    if s == 0:
                        pe.wait_ge(hs_lo_ok, CH * k + c + 1)
                    elif c == 0:
                        pe.wait_ge(hs_lo_ok, CH * k + CH)
                    last = product3(span(psY, s), W2_hi[:, s, c, :], W2_lo[:, s, c, :],
                                    span(hs_hi[:, half(par, s), c, :], s), span(hs_lo[:, half(par, s), c, :], s),
                                    s == 0 and c == 0, s == NS - 1 and c == CH - 1)
                last.then_inc(down_ok, 1)

            def tile(t, par, last=False):
                for s in range(NS):
                    down(t, par, s)
                    if s < NS - 2:
                        up(t, par, s + 2)
                    elif not last:
                        up(t + 1, 1 - par, s + 2 - NS)
                pe.wait_ge(outT_ok, t + 1)
                pe.wait_ge(out_tok_ok, t)
                for b in range(NB):
                    tr = nc.tensor.transpose(psOut[:, b * D:(b + 1) * D], outT[:, b * L:(b + 1) * L], ident[:, :])
                tr.then_inc(out_ps, 1)

            pe.wait_ge(segsum_ok, 3 * NT)
            pe.wait_ge(mod_ok, 1)
            for i in range(3):
                last = nc.tensor.matmul(psLogit, segsum[:, i, :], gw[:, i, :], start=(i == 0), stop=(i == 2))
            last.then_inc(logit_ps, 1)
            pe.wait_ge(x1_lo_ok, NT)
            up(0, 0, 0)
            up(0, 0, 1)
            pe.wait_ge(w_ok, 2)
            nc.tensor.matmul(psBcast, ones[:, :], w_diag[:, :, :].rearrange("p b e -> p (b e)"),
                             start=True, stop=True)
            nc.tensor.matmul(psWgtT, gt[:, 15, 0:E], ident[0:B, 0:B], start=True, stop=True).then_inc(w_bcast_ps, 1)
            pe.wait_ge(w_all_ok, 1)
            pe.wait_ge(wT_seg_ok, 3)
            nc.tensor.matmul(psBias, eb2_raw[:, :], wT_seg[:, :, :].rearrange("e s b -> e (s b)"),
                             start=True, stop=True).then_inc(bias_ps, 1)
            with pe.Fori(0, NT - 2, 2) as t:
                tile(t, 0)
                tile(t + 1, 1)
            tile(NT - 2, 0)
            tile(NT - 1, 1, last=True)

        @block.vector
        def _(dve):
            n_gate = 0

            def linked(ins):
                nonlocal n_gate
                n_gate += 1
                ins.then_inc(gate_step, 1)
                dve.wait_ge(gate_step, n_gate)

            dve.wait_ge(zmask_ok, 1)
            for i in range(2):
                nc.vector.tensor_copy(z1_hi[ZR:KR, i, :], zmask[ZR:KR, :, :].rearrange("p b l -> p (b l)")
                                      ).then_inc(zbias_rows, 1)
                nc.vector.memset(f32(z1_lo[ZR:KR, i, :]), 0.0).then_inc(zbias_rows, 1)
            dve.wait_ge(WT_hi_ok, 1)
            nc.vector.tensor_tensor(WT_lo[:, :], psWT, f32(WT_hi[:, :]), ALU.subtract).then_inc(WT_lo_ok, 1)

            def xT_low(t):
                dve.wait_ge(xT_hi_ok, t + 1)
                if t >= 2:
                    dve.wait_ge(y0_ps, t - 1)
                nc.vector.tensor_tensor(xT_lo[:, t % 2, :], psA[t % 2], f32(xT_hi[:, t % 2, :]),
                                        ALU.subtract).then_inc(xT_lo_ok, 1)

            def mask_z1(t):
                dve.wait_ge(z_ps, t + 1)
                if t >= 2:
                    dve.wait_ge(z1_lo_ok, t - 1)
                nc.vector.tensor_tensor(z1[:, t % 2, :], psZ[t % 2], zmask[0:ZR, :, :].rearrange("p b l -> p (b l)"),
                                        ALU.mult).then_inc(z1_ok, 1)

            def residual0(t):
                dve.wait_ge(g0_ok, t + 1)
                c = slice(t * TOK, (t + 1) * TOK)
                nc.vector.tensor_tensor(x1[:, c], psA[t % 2], g0[:, t % 2, :], ALU.add).then_inc(x1_ok, 1)
                dve.wait_ge(x1_ok, t + 1)
                x1v = x1[:, c].rearrange("p (b l) -> p b l", l=L)
                for i, (at, _, n) in enumerate(SEGS):
                    nc.vector.tensor_reduce(segsum[:, i, t * NB:(t + 1) * NB], x1v[:, :, at:at + n], AX.X,
                                            ALU.add).then_inc(segsum_ok, 1)

            for s in range(NT + 3):
                if 0 <= s - 2 < NT:
                    residual0(s - 2)
                if 0 <= s - 1 < NT:
                    mask_z1(s - 1)
                if s < NT:
                    xT_low(s)
                if s == 0:
                    dve.wait_ge(F_in, 16)
                    nc.vector.tensor_copy(F_hi[:, :], F_raw[:, :]).then_inc(F_hi_ok, 1)
                    dve.wait_ge(F_hi_ok, 1)
                    nc.vector.tensor_tensor(F_lo[:, :], F_raw[:, :], f32(F_hi[:, :]), ALU.subtract
                                            ).then_inc(F_lo_ok, 1)
                    dve.wait_ge(fT_hi_ok, 3)
                    nc.vector.tensor_tensor(fT_lo[ZR:KR, :, :], cond_rows[ZR:KR, :, :], f32(fT_hi[ZR:KR, :, :]),
                                            ALU.subtract).then_inc(fT_lo_ok, 1)
                    for i in range(2):
                        ts = slice(i * NT // 2, (i + 1) * NT // 2)
                        nc.vector.tensor_tensor(fT_lo[0:ZR, ts, :], psFT[i].rearrange("p (t d) -> p t d", d=D),
                                                f32(fT_hi[0:ZR, ts, :]), ALU.subtract).then_inc(fT_lo_ok, 1)
                if s == 4:
                    dve.wait_ge(small_in, 16 * 6)
                    dve.wait_ge(tanh_c_ok, 1)
                    nc.vector.scalar_tensor_tensor(silu2[:, :], tanh_c[:, :], 1.0, psCondT, ALU.add,
                                                   ALU.mult).then_inc(silu_ok, 1)
                    nc.vector.tensor_scalar(tw[:, :], time_w_raw[:, :], 0.5, None, ALU.mult).then_inc(gate_consts, 1)
                if s == 5:
                    inv = 1.0 / (HEAD + PROP)
                    linked(nc.vector.tensor_scalar(gw[:, 3, :], gate_raw[:, 0, :], 1.0 / L, None, ALU.mult))
                    linked(nc.vector.scalar_tensor_tensor(gw[:, 0, :], gate_raw[:, 1, :], inv, gw[:, 3, :],
                                                          ALU.mult, ALU.add))
                    linked(nc.vector.scalar_tensor_tensor(gw[:, 2, :], gate_raw[:, 2, :], inv, gw[:, 3, :],
                                                          ALU.mult, ALU.add))
                    linked(nc.vector.scalar_tensor_tensor(gw[:, 1, :], gate_raw[:, 2, :], inv, gw[:, 0, :],
                                                          ALU.mult, ALU.add))

            def split(t, par, s):
                k = NS * t + s
                if not isinstance(k, int) or k >= 1:
                    dve.wait_ge(down_ok, k - 1)
                hb, hi, lo = h[:, half(par, s), :, :], hs_hi[:, half(par, s), :, :], hs_lo[:, half(par, s), :, :]
                if s == 0:
                    for c in range(CH):
                        dve.wait_ge(h_ok, CH * k + c + 1)
                        nc.vector.tensor_copy(hi[:, c, :], hb[:, c, :]).then_inc(hs_hi_ok, 1)
                        dve.wait_ge(hs_hi_ok, CH * k + c + 1)
                        nc.vector.tensor_tensor(lo[:, c, :], hb[:, c, :], f32(hi[:, c, :]), ALU.subtract
                                                ).then_inc(hs_lo_ok, 1)
                    return
                a, z = SPAN[s]
                dve.wait_ge(h_ok, CH * (k + 1))
                for b in range(NB):
                    c = slice(b * L + a, b * L + z)
                    nc.vector.tensor_scalar(hi[:, :, c], hb[:, :, c], w_tile[:, b * E + s - 1:b * E + s], None,
                                            ALU.mult).then_inc(hs_hi_ok, 1)
                for b in range(NB):
                    c = slice(b * L + a, b * L + z)
                    dve.wait_ge(hs_hi_ok, CH * k + b + 1)
                    nc.vector.scalar_tensor_tensor(lo[:, :, c], hb[:, :, c], w_tile[:, b * E + s - 1:b * E + s],
                                                   f32(hi[:, :, c]), ALU.mult, ALU.subtract).then_inc(hs_lo_ok, 1)

            def tile(t, par, last=False):
                nc.vector.tensor_copy(w_tile[:, :], w_all[:, bass.ds(t * NB * E, NB * E)]).then_inc(w_tile_ok, 1)
                dve.wait_ge(w_tile_ok, t + 1)
                for s in range(1, NS):
                    split(t, par, s)
                if not last:
                    split(t + 1, 1 - par, 0)
                dve.wait_ge(down_ok, NS * (t + 1))
                nc.vector.tensor_tensor(outT[:, :], psY, x1[:, bass.ds(t * TOK, TOK)], ALU.add).then_inc(outT_ok, 1)

            dve.wait_ge(mod_ps, 1)
            nc.vector.tensor_tensor(gt[:, 0, :], psMod, time_b_row[:, :], ALU.add).then_inc(mod_ok, 1)
            dve.wait_ge(mod_ok, 1)
            linked(nc.vector.tensor_scalar(gt[:, 1, 0:E], gt[:, 0, 0:E], 1.0, None, ALU.add))
            split(0, 0, 0)
            dve.wait_ge(logit_ps, 1)
            lg, ex = gt[:, 2, 0:E], gt[:, 7, 0:E]
            linked(nc.vector.tensor_tensor(lg, psLogit, gate_b_row[:, :], ALU.add))
            linked(nc.vector.tensor_tensor(lg, lg, gt[:, 1, 0:E], ALU.mult))
            linked(nc.vector.tensor_tensor(lg, lg, gt[:, 0, E:2 * E], ALU.add))
            linked(nc.vector.tensor_reduce(gt[:, 14, 0:1], lg, AX.X, ALU.max))
            nc.vector.tensor_scalar(gt[:, 3, 0:E], lg, gt[:, 14, 0:1], None, ALU.subtract).then_inc(gate_x, 1)
            lg_e = lg.unsqueeze(2).to_broadcast([B, E, E])
            lg_j = lg.unsqueeze(1).to_broadcast([B, E, E])
            nc.vector.tensor_tensor(cmp_gt[:, :, :], lg_j, lg_e, ALU.is_gt)
            dve.wait_ge(gate_consts, 5)
            linked(nc.vector.tensor_tensor(cmp_eq[:, :, :], lg_j, lg_e, ALU.is_equal))
            linked(nc.vector.tensor_tensor(cmp_eq[:, :, :], cmp_eq[:, :, :], before[:, :, :], ALU.mult))
            linked(nc.vector.tensor_tensor(cmp_gt[:, :, :], cmp_gt[:, :, :], cmp_eq[:, :, :], ALU.add))
            linked(nc.vector.tensor_reduce(gt[:, 8, 0:E], cmp_gt[:, :, :], AX.X, ALU.add))
            linked(nc.vector.tensor_scalar(gt[:, 9, 0:E], gt[:, 8, 0:E], 1.5, None, ALU.is_lt))
            dve.wait_ge(gate_tanh, 1)
            nc.vector.tensor_scalar(gt[:, 5, 0:E], gt[:, 4, 0:E], 1.0, None, ALU.add)
            linked(nc.vector.tensor_scalar(gt[:, 6, 0:E], gt[:, 4, 0:E], -1.0, 1.0, ALU.mult, ALU.add))
            linked(nc.vector.reciprocal(gt[:, 6, 0:E], gt[:, 6, 0:E]))
            linked(nc.vector.tensor_tensor(ex, gt[:, 5, 0:E], gt[:, 6, 0:E], ALU.mult))
            linked(nc.vector.tensor_reduce(gt[:, 10, 0:1], ex, AX.X, ALU.add))
            linked(nc.vector.reciprocal(gt[:, 11, 0:1], gt[:, 10, 0:1]))
            linked(nc.vector.scalar_tensor_tensor(gt[:, 12, 0:E], ex, gt[:, 11, 0:1], gt[:, 9, 0:E],
                                                  ALU.mult, ALU.mult))
            linked(nc.vector.tensor_reduce(gt[:, 13, 0:1], gt[:, 12, 0:E], AX.X, ALU.add))
            linked(nc.vector.tensor_scalar(gt[:, 13, 0:1], gt[:, 13, 0:1], 1e-8, None, ALU.add))
            linked(nc.vector.reciprocal(gt[:, 13, 0:1], gt[:, 13, 0:1]))
            nc.vector.tensor_scalar(gt[:, 15, 0:E], gt[:, 12, 0:E], gt[:, 13, 0:1], None, ALU.mult).then_inc(w_ok, 1)
            dve.wait_ge(w_ok, 1)
            nc.vector.tensor_tensor(w_diag[:, :, :], own_batch[:, :, :],
                                    gt[:, 15, 0:E].unsqueeze(1).to_broadcast([B, B, E]), ALU.mult).then_inc(w_ok, 1)
            dve.wait_ge(w_bcast_ps, 1)
            nc.vector.tensor_copy(w_all[:, :], psBcast).then_inc(w_all_ok, 1)
            for i in range(3):
                nc.vector.tensor_scalar(wT_seg[:, i, :], psWgtT, seg_mask[:, i:i + 1], None, ALU.mult
                                        ).then_inc(wT_seg_ok, 1)
            dve.wait_ge(bias_ps, 1)
            nc.vector.tensor_scalar(bias2[:, :, :].rearrange("p s b -> p (s b)"), psBias, sb2_col[:, 0:1], None,
                                    ALU.add).then_inc(bias_ok, 1)
            dve.wait_ge(w_all_ok, 1)
            dve.wait_ge(x1b_ok, 3)
            with dve.Fori(0, NT - 2, 2) as t:
                tile(t, 0)
                tile(t + 1, 1)
            tile(NT - 2, 0)
            tile(NT - 1, 1, last=True)


_INS = ["x", "fside_Bx1x1024x16_0", "cond_1024", "L0_cond_W", "L0_cond_fc_bias", "L1_cond_gate_w", "L1_cond_gate_b",
        "L1_cond_time_w", "L1_cond_time_b", "L1_cond_ew1", "L1_cond_eb1", "L1_cond_ew2", "L1_cond_eb2",
        "L1_cond_sw1", "L1_cond_sb1", "L1_cond_sw2", "L1_cond_sb2"]


def kernel(**inputs):
    import numpy as np
    import concourse.bacc as bacc
    from concourse.bass_utils import run_bass_kernel_spmd

    nc = bacc.Bacc("TRN2", target_bir_lowering=False, num_devices=1)
    arrays, args = {}, []
    for name in _INS:
        a = np.ascontiguousarray(inputs[name])
        arrays[f"in_{name}"] = a
        args.append(nc.dram_tensor(f"in_{name}", a.shape, mybir.dt.from_np(a.dtype), kind="ExternalInput").ap())
    shape = arrays["in_x"].shape
    args.append(nc.dram_tensor("out_0", shape, F32, kind="ExternalOutput").ap())
    build(nc, *args)
    r = run_bass_kernel_spmd(nc, [arrays], core_ids=[0])
    return r.results[0]["out_0"]
```

```python
from contextlib import ExitStack

import concourse.bass as bass
from concourse import mybir

F32 = mybir.dt.float32
F32R = mybir.dt.float32r
ALU = mybir.AluOpType
ACT = mybir.ActivationFunctionType
AX = mybir.AxisListType


def build(nc, x, fside, cond, W, fc_bias, gate_w, gate_b, time_w, time_b,
          ew1, eb1, ew2, eb2, sw1, sb1, sw2, sb2, out):
    B, L, D = x.shape
    R = fside.shape[-1]
    E, _, H = ew1.shape
    NB = 4
    NT = B // NB
    TOK = NB * L
    CH = H // 128
    HEAD = L // 3
    PROP = L - 2 * HEAD
    SEGS = [(0, 0, HEAD), (HEAD, 2 * HEAD, PROP), (HEAD + PROP, HEAD, HEAD)]
    NSEG = len(SEGS)
    NS = E + 1
    SPAN = [(0, L), (0, L), (0, HEAD + PROP), (HEAD, L), (0, L)]
    Z_SCALE = 1.0 / (D * R)
    ZR = NB * R
    KR = ZR + NB
    UP = 5
    BANK_Y, BANK_OUT, BANK_L0 = 5, 6, 7
    W_ORDER = (0, 2, 1, 4, 3, 6, 5, 8, 7, 9)
    GATE_LINKS = 14

    with ExitStack() as ctx:
        def sb(name, shape, dt=F32):
            return ctx.enter_context(nc.sbuf_tensor(name, shape, dt))

        def sem(name):
            return ctx.enter_context(nc.semaphore(name))

        ps = ctx.enter_context(nc.psum_tensor("ps", [128, 8, 512], F32))

        x_tok = sb("x_tok", [128, 2, NB, D])
        F_raw = sb("F_raw", [128, 2, ZR])
        cond_rows = sb("cond_rows", [KR, 2, D])
        W_raw = sb("W_raw", [128, D])
        cond_raw = sb("cond_raw", [B, D])
        fcb = sb("fcb", [128, 1])
        sb2_col = sb("sb2_col", [128, 1])
        gate_raw = sb("gate_raw", [128, 3, E])
        gate_b_row = sb("gate_b_row", [128, E])
        time_w_raw = sb("time_w_raw", [128, 2 * E])
        time_b_row = sb("time_b_row", [128, 2 * E])
        eb2_raw = sb("eb2_raw", [E, D])
        b1_col = sb("b1_col", [128, NS, CH])
        W1_raw = sb("W1_raw", [128, NS, H])
        W2_raw = sb("W2_raw", [128, NS, H])
        ident = sb("ident", [128, 128])
        ones = sb("ones", [128, 128])
        zmask = sb("zmask", [KR, NB, L])
        before = sb("before", [128, NB, E, E])
        WT_hi = sb("WT_hi", [128, D], F32R)
        WT_lo = sb("WT_lo", [128, D], F32R)
        W1_hi = sb("W1_hi", [128, NS, CH, 128], F32R)
        W1_lo = sb("W1_lo", [128, NS, CH, 128], F32R)
        W2_hi = sb("W2_hi", [128, NS, CH, 128], F32R)
        W2_lo = sb("W2_lo", [128, NS, CH, 128], F32R)
        F_hi = sb("F_hi", [128, ZR], F32R)
        F_lo = sb("F_lo", [128, ZR], F32R)
        fT_hi = sb("fT_hi", [KR, D], F32R)
        fT_lo = sb("fT_lo", [KR, D], F32R)
        xT_hi = sb("xT_hi", [128, TOK], F32R)
        xT_lo = sb("xT_lo", [128, TOK], F32R)
        z1 = sb("z1", [ZR, TOK])
        z1_hi = sb("z1_hi", [KR, TOK], F32R)
        z1_lo = sb("z1_lo", [KR, TOK], F32R)
        g0 = sb("g0", [128, TOK])
        x1 = sb("x1", [128, 2, TOK])
        x1_hi = sb("x1_hi", [128, 2, TOK], F32R)
        x1_lo = sb("x1_lo", [128, 2, TOK], F32R)
        tanh_c = sb("tanh_c", [128, B])
        silu2 = sb("silu2", [128, B])
        tw = sb("tw", [128, 2 * E])
        mod_terms = sb("mod_terms", [128, B, 2 * E])
        mod = sb("mod", [128, B, 2 * E])
        gate_mul = sb("gate_mul", [128, B, E])
        gate_add = sb("gate_add", [128, B, E])
        gw_full = sb("gw_full", [128, E])
        gw = sb("gw", [128, NSEG, E])
        eb2T = sb("eb2T", [128, NSEG, E])
        segsum = sb("segsum", [128, NSEG, NB])
        gate_terms = sb("gate_terms", [128, NSEG, NB, E])
        gate_fold = sb("gate_fold", [128, NB, E])
        logit = sb("logit", [128, NB, E])
        logit_x = sb("logit_x", [128, NB, E])
        top = sb("top", [128, NB])
        tanh_g = sb("tanh_g", [128, NB, E])
        numer = sb("numer", [128, NB, E])
        denom = sb("denom", [128, NB, E])
        expd = sb("expd", [128, NB, E])
        exp_top = sb("exp_top", [128, NB, E])
        greater = sb("greater", [128, NB, E, E])
        equal = sb("equal", [128, NB, E, E])
        rank = sb("rank", [128, NB, E])
        chosen = sb("chosen", [128, NB, E])
        sum_all = sb("sum_all", [128, NB])
        sum_top = sb("sum_top", [128, NB])
        w_be = sb("w_be", [128, NB, E])
        bias_terms = sb("bias_terms", [128, NSEG, NB, E])
        bias2 = sb("bias2", [128, NSEG, NB])
        h = sb("h", [128, 2, CH, TOK])
        hs_hi = sb("hs_hi", [128, 2, CH, TOK], F32R)
        hs_lo = sb("hs_lo", [128, 2, CH, TOK], F32R)
        outT = sb("outT", [128, TOK])
        out_tok = sb("out_tok", [128, NB, D])
        table_probe = sb("table_probe", [128, 3])

        x_in = [sem("x_in_even"), sem("x_in_odd")]
        F_in = [sem("F_in_even"), sem("F_in_odd")]
        rows_in = [sem("rows_in_even"), sem("rows_in_odd")]
        W_in, cond_in, fcb_in, small_in, b1_in = (sem("W_in"), sem("cond_in"), sem("fcb_in"), sem("small_in"),
                                                  sem("b1_in"))
        w_in = [sem(f"w_in{n}") for n in range(2 * NS)]
        probe_ok, hi4_ok = sem("probe_ok"), sem("hi4_ok")
        const_step, ident_ok, ones_ok, zmask_ok, before_ok = (sem("const_step"), sem("ident_ok"), sem("ones_ok"),
                                                              sem("zmask_ok"), sem("before_ok"))
        zbias_ok, WT_ps, condT_ps, eb2T_ps, WT_hi_ok, WT_lo_ok = (
            sem("zbias_ok"), sem("WT_ps"), sem("condT_ps"), sem("eb2T_ps"), sem("WT_hi_ok"), sem("WT_lo_ok"))
        w_hi_ok, w_lo_dve, w_lo_pool = sem("w_hi_ok"), sem("w_lo_dve"), sem("w_lo_pool")
        tanh_c_ok, setup_step, mod_terms_ok, mod_ps, mod_read, silu_ok, eb2T_read = (
            sem("tanh_c_ok"), sem("setup_step"), sem("mod_terms_ok"), sem("mod_ps"), sem("mod_read"),
            sem("silu_ok"), sem("eb2T_read"))
        xT_ps, x_fp_ok, xT_hi_ok, xT_lo_ok = sem("xT_ps"), sem("x_fp_ok"), sem("xT_hi_ok"), sem("xT_lo_ok")
        F_hi_ok, F_lo_ok, fT_ps, fT_hi_ok, fT_lo_ok = (sem("F_hi_ok"), sem("F_lo_ok"), sem("fT_ps"),
                                                       sem("fT_hi_ok"), sem("fT_lo_ok"))
        z_ps, z1_ok, z1_hi_ok, z1_lo_ok = sem("z_ps"), sem("z1_ok"), sem("z1_hi_ok"), sem("z1_lo_ok")
        y0_ps, g0_ok, x1_ok, x1_hi_ok, x1_lo_ok = (sem("y0_ps"), sem("g0_ok"), sem("x1_ok"), sem("x1_hi_ok"),
                                                   sem("x1_lo_ok"))
        gate_fold_ok = sem("gate_fold_ok")
        segsum_ok, gate_terms_ok, logit_ps, logit_read = (sem("segsum_ok"), sem("gate_terms_ok"), sem("logit_ps"),
                                                          sem("logit_read"))
        gate_step, logit_x_ok, tanh_g_ok, w_ok, bias2_ok, x1b_ok = (
            sem("gate_step"), sem("logit_x_ok"), sem("tanh_g_ok"), sem("w_ok"), sem("bias2_ok"), sem("x1b_ok"))
        up_ps, h_ok, shared_lo_ok, hi_ok, lo_ok, down_ok = (
            sem("up_ps"), sem("h_ok"), sem("shared_lo_ok"), sem("hi_ok"), sem("lo_ok"), sem("down_ok"))
        outT_ok, out_ps, out_tok_ok, out_left = sem("outT_ok"), sem("out_ps"), sem("out_tok_ok"), sem("out_left")

        psL0 = ps[:, BANK_L0, :]
        psZ = ps[0:ZR, BANK_L0, :]
        psLogit = ps[:, BANK_L0, 0:NB * E].rearrange("p (b e) -> p b e", e=E)
        psFT = ps[0:ZR, BANK_OUT, 0:D]
        psOut = ps[:, BANK_OUT, :]
        psY = ps[:, BANK_Y, :]
        psWT, psCondT, psEb2T = ps[:, 0, 0:D], ps[:, 1, 0:B], ps[:, BANK_Y, 0:E]
        psMod = ps[:, BANK_OUT, 0:B * 2 * E].rearrange("p (b e) -> p b e", e=2 * E)

        block = ctx.enter_context(nc.Block())

        def f32(ap):
            return ap.bitcast(F32)

        def span(ap, s):
            a, z = SPAN[s]
            return ap if z - a == L else ap.rearrange("p (b l) -> p b l", l=L)[:, :, a:z]

        def half(par, s):
            return (NS * par + s) % 2

        def up_bank(s, c):
            a, z = SPAN[s]
            bank = ps[:, (s * CH + c) % UP, 0:NB * (z - a)]
            return bank if z - a == L else bank.rearrange("p (b l) -> p b l", b=NB)

        def arrivals(t, par, each):
            return (t - par) * (each // 2) + each

        def weight(n):
            e = n // 2
            if n % 2 == 0:
                return W1_raw[:, e, :].rearrange("p (m c) -> p c m", c=CH), W1_hi[:, e, :, :], W1_lo[:, e, :, :]
            return W2_raw[:, e, :].rearrange("p (c m) -> p c m", c=CH), W2_hi[:, e, :, :], W2_lo[:, e, :, :]

        def wait_weight_lo(eng, n):
            eng.wait_ge(w_lo_pool if n % 2 else w_lo_dve, n // 2 + 1)

        def make_weight_lo(eng, n):
            eng.wait_ge(w_hi_ok, W_ORDER.index(n) + 1)
            raw, hi, lo = weight(n)
            eng.tensor_tensor(lo, raw, f32(hi), ALU.subtract).then_inc(w_lo_pool if n % 2 else w_lo_dve, 1)

        @block.sync
        def _(sp):
            def load(t, par):
                b = t * NB
                for at, src, n in SEGS:
                    sp.dma_start(x_tok[at:at + n, par, :, :],
                                 x[bass.ds(b, NB), src:src + n, :].rearrange("b l d -> l b d")
                                 ).then_inc(x_in[par], 16)
                sp.dma_start(F_raw[:, par, :].rearrange("i (b r) -> i b r", r=R),
                             fside[bass.ds(b, NB), 0, :, :].rearrange("b i r -> i b r")).then_inc(F_in[par], 16)
                sp.dma_start(cond_rows[ZR:KR, par, :], cond[bass.ds(b, NB), :]).then_inc(rows_in[par], 16)

            def store(t):
                sp.wait_ge(out_tok_ok, t + 1)
                for at, dst, n in SEGS:
                    sp.dma_start(out[bass.ds(t * NB, NB), dst:dst + n, :].rearrange("b l d -> l b d"),
                                 out_tok[at:at + n, :, :]).then_inc(out_left, 16)

            def tile(t, par):
                sp.wait_ge(xT_ps, t + 1)
                sp.wait_ge(F_lo_ok, t + 1)
                sp.wait_ge(fT_lo_ok, 2 * t + 2)
                load(t + 2, par)
                store(t)

            def load_weight(n):
                e = n // 2
                if n % 2 == 0:
                    sp.dma_start(W1_raw[:, e, :], sw1 if e == 0 else ew1[e - 1]).then_inc(w_in[n], 16)
                else:
                    src = sw2 if e == 0 else ew2[e - 1]
                    sp.dma_start(W2_raw[:, e, :], src.rearrange("(p c) d -> p (c d)", c=CH)).then_inc(w_in[n], 16)

            load(0, 0)
            for n in W_ORDER[:3]:
                load_weight(n)
            sp.dma_start(b1_col[:, 1:NS, :], eb1.rearrange("e (p c) -> p e c", c=CH)).then_inc(b1_in, 16)
            sp.dma_start(b1_col[:, 0, :], sb1.rearrange("(p c) -> p c", c=CH)).then_inc(b1_in, 16)
            for n in W_ORDER[3:]:
                load_weight(n)
            load(1, 1)
            with sp.Fori(0, NT - 3, 2) as t:
                tile(t, 0)
                tile(t + 1, 1)
            store(NT - 2)
            store(NT - 1)
            sp.wait_ge(out_left, 16 + 16 * NSEG * NT)

        @block.gpsimd
        def _(pool):
            n_const = 0

            def chained(ins):
                nonlocal n_const
                n_const += 1
                ins.then_inc(const_step, 1)
                pool.wait_ge(const_step, n_const)

            nc.gpsimd.memset(table_probe[:, :], 0.0).then_inc(probe_ok, 1)
            chained(nc.gpsimd.memset(ident[:, :], 0.0))
            nc.gpsimd.affine_select(out=ident[:, :], in_=ident[:, :], compare_op=ALU.not_equal, fill=1.0, base=0,
                                    pattern=[[-1, 128]], channel_multiplier=1).then_inc(ident_ok, 1)
            chained(nc.gpsimd.memset(zmask[:, :, :], Z_SCALE))
            chained(nc.gpsimd.affine_select(out=zmask[:, :, :], in_=zmask[:, :, :], compare_op=ALU.is_ge, fill=0.0,
                                            base=0, pattern=[[-R, NB], [0, L]], channel_multiplier=1))
            chained(nc.gpsimd.affine_select(out=zmask[:, :, :], in_=zmask[:, :, :], compare_op=ALU.is_ge, fill=0.0,
                                            base=R - 1, pattern=[[R, NB], [0, L]], channel_multiplier=-1))
            nc.gpsimd.affine_select(out=zmask[:, :, :], in_=zmask[:, :, :], compare_op=ALU.not_equal, fill=1.0,
                                    base=-ZR, pattern=[[-1, NB], [0, L]], channel_multiplier=1).then_inc(zmask_ok, 1)
            for dst, src in (
                    (gate_raw[:, :, :], gate_w.rearrange("(g d) e -> d g e", g=3)),
                    (time_w_raw[:, :], time_w),
                    (gate_b_row[:, :], gate_b.rearrange("(a e) -> a e", a=1).to_broadcast([128, E])),
                    (time_b_row[:, :], time_b.rearrange("(a e) -> a e", a=1).to_broadcast([128, 2 * E])),
                    (eb2_raw[:, :], eb2),
                    (sb2_col[:, :], sb2.rearrange("(p a) -> p a", a=1))):
                pool.dma_start(dst, src).then_inc(small_in, 16)
            nc.gpsimd.memset(ones[:, :], 1.0).then_inc(ones_ok, 1)
            chained(nc.gpsimd.memset(before[:, :, :, :], 1.0))
            nc.gpsimd.affine_select(out=before[:, :, :, :], in_=before[:, :, :, :], compare_op=ALU.is_ge, fill=0.0,
                                    base=-1, pattern=[[0, NB], [1, E], [-1, E]], channel_multiplier=0
                                    ).then_inc(before_ok, 1)

            def xT_low(t, par):
                pool.wait_ge(x_fp_ok, t + 1)
                pool.wait_ge(xT_hi_ok, t + 1)
                nc.gpsimd.tensor_tensor(xT_lo[:, :], x1[:, par, :], f32(xT_hi[:, :]), ALU.subtract
                                        ).then_inc(xT_lo_ok, 1)

            def z1_low(t):
                pool.wait_ge(z1_hi_ok, t + 1)
                nc.gpsimd.tensor_tensor(z1_lo[0:ZR, :], z1[:, :], f32(z1_hi[0:ZR, :]), ALU.subtract
                                        ).then_inc(z1_lo_ok, 1)

            def output_bias(t, par):
                pool.wait_ge(bias2_ok, t + 1)
                xb = x1[:, par, :].rearrange("p (b l) -> p b l", l=L)
                for i, (at, _, n) in enumerate(SEGS):
                    nc.gpsimd.tensor_tensor(xb[:, :, at:at + n], xb[:, :, at:at + n],
                                            bias2[:, i, :].unsqueeze(2).to_broadcast([128, NB, n]),
                                            ALU.add).then_inc(x1b_ok, 1)

            def shared_low(t, par):
                k = NS * t
                for c in range(CH):
                    pool.wait_ge(h_ok, CH * k + c + 1)
                    hf = half(par, 0)
                    nc.gpsimd.tensor_tensor(hs_lo[:, hf, c, :], h[:, hf, c, :], f32(hs_hi[:, hf, c, :]),
                                            ALU.subtract).then_inc(shared_lo_ok, 1)

            def tile(t, par, last=False):
                if not last:
                    xT_low(t + 1, 1 - par)
                output_bias(t, par)
                if not last:
                    z1_low(t + 1)
                    shared_low(t + 1, 1 - par)

            for n in W_ORDER:
                if n % 2:
                    make_weight_lo(pool, n)
            shared_low(0, 0)
            with pool.Fori(0, NT - 3, 2) as t:
                tile(t, 0)
                tile(t + 1, 1)
            tile(NT - 2, 0)
            tile(NT - 1, 1, last=True)

        @block.scalar
        def _(act):
            act.sem_inc(out_left, 16)
            act.dma_start(W_raw[:, :], W).then_inc(W_in, 16)
            act.dma_start(fcb[:, :], fc_bias.rearrange("(p a) -> p a", a=1)).then_inc(fcb_in, 16)
            act.dma_start(cond_raw[:, :], cond).then_inc(cond_in, 16)

            def weight_high(n):
                act.wait_ge(w_in[n], 16)
                raw, hi, _ = weight(n)
                nc.scalar.activation(hi, raw, ACT.Copy).then_inc(w_hi_ok, 1)

            def xT_copies(t, par):
                act.wait_ge(xT_ps, t + 1)
                nc.scalar.activation(x1[:, par, :], psL0, ACT.Copy).then_inc(x_fp_ok, 1)
                nc.scalar.activation(xT_hi[:, :], psL0, ACT.Copy).then_inc(xT_hi_ok, 1)

            def fT_high(t, par):
                act.wait_ge(rows_in[par], arrivals(t, par, 16))
                nc.scalar.activation(fT_hi[ZR:KR, :], cond_rows[ZR:KR, par, :], ACT.Copy)
                act.wait_ge(fT_ps, t + 1)
                nc.scalar.activation(fT_hi[0:ZR, :], psFT, ACT.Copy).then_inc(fT_hi_ok, 1)

            def z1_high(t):
                act.wait_ge(z1_ok, t + 1)
                nc.scalar.activation(z1_hi[0:ZR, :], z1[:, :], ACT.Copy).then_inc(z1_hi_ok, 1)

            def gelu0(t):
                act.wait_ge(y0_ps, t + 1)
                nc.scalar.activation(g0[:, :], psL0, ACT.Gelu, bias=fcb[:, 0:1]).then_inc(g0_ok, 1)

            def preload_gelu(t):
                act.wait_ge(probe_ok, t + 1)
                nc.scalar.activation(table_probe[:, 1:2], table_probe[:, 0:1], ACT.Gelu).then_inc(probe_ok, 1)

            def expert4_high(t, par):
                act.wait_ge(w_ok, t + 1)
                act.wait_ge(h_ok, CH * (NS * t + NS))
                for b in range(NB):
                    c = slice(b * L, (b + 1) * L)
                    hf = half(par, NS - 1)
                    nc.scalar.activation(hs_hi[:, hf, :, c], h[:, hf, :, c], ACT.Copy, scale=w_be[:, b, E - 1:E]
                                         ).then_inc(hi4_ok, 1)

            def gate_tanh(t):
                act.wait_ge(logit_x_ok, t + 1)
                nc.scalar.activation(tanh_g[:, :, :], logit_x[:, :, :], ACT.Tanh, scale=0.5).then_inc(tanh_g_ok, 1)

            def gelu(t, par, s):
                k = NS * t + s
                for c in range(CH):
                    act.wait_ge(up_ps, CH * k + c + 1)
                    hf = half(par, s)
                    dst = span(h[:, hf, c, :], s)
                    ins = nc.scalar.activation(dst, up_bank(s, c), ACT.Gelu_apprx_tanh, bias=b1_col[:, s, c:c + 1])
                    if s == 0:
                        ins = nc.scalar.activation(hs_hi[:, hf, c, :], up_bank(s, c), ACT.Gelu_apprx_tanh,
                                                   bias=b1_col[:, s, c:c + 1])
                    ins.then_inc(h_ok, 1)

            def tile(t, par, last=False):
                if not last:
                    xT_copies(t + 1, 1 - par)
                gelu(t, par, 2)
                if not last:
                    fT_high(t + 1, 1 - par)
                    z1_high(t + 1)
                gelu(t, par, 3)
                if not last:
                    preload_gelu(t + 1)
                    gelu0(t + 1)
                gelu(t, par, 4)
                expert4_high(t, par)
                if not last:
                    gelu(t + 1, 1 - par, 0)
                    gate_tanh(t + 1)
                    gelu(t + 1, 1 - par, 1)
                act.wait_ge(out_ps, t + 1)
                act.wait_ge(out_left, 16 * NSEG * t + 16)
                nc.scalar.activation(out_tok[:, :, :], psOut.rearrange("p (b d) -> p b d", d=D),
                                     ACT.Copy).then_inc(out_tok_ok, 1)

            xT_copies(0, 0)
            act.wait_ge(WT_ps, 1)
            nc.scalar.activation(WT_hi[:, :], psWT, ACT.Copy).then_inc(WT_hi_ok, 1)
            fT_high(0, 0)
            weight_high(W_ORDER[0])
            z1_high(0)
            act.wait_ge(condT_ps, 1)
            nc.scalar.activation(tanh_c[:, :], psCondT, ACT.Tanh, scale=0.5).then_inc(tanh_c_ok, 1)
            for n in W_ORDER[1:5]:
                weight_high(n)
            act.wait_ge(fcb_in, 16)
            preload_gelu(0)
            gelu0(0)
            nc.scalar.activation(table_probe[:, 2:3], table_probe[:, 0:1], ACT.Gelu_apprx_tanh)
            for n in W_ORDER[5:]:
                weight_high(n)
            act.wait_ge(b1_in, 32)
            gelu(0, 0, 0)
            gate_tanh(0)
            gelu(0, 0, 1)
            with act.Fori(0, NT - 3, 2) as t:
                tile(t, 0)
                tile(t + 1, 1)
            tile(NT - 2, 0)
            tile(NT - 1, 1, last=True)

        @block.tensor
        def _(pe):
            def product3(dst, w_hi, w_lo, m_hi, m_lo, start, stop):
                nc.tensor.matmul(dst, w_hi, m_hi, start=start, stop=False)
                nc.tensor.matmul(dst, w_hi, m_lo, start=False, stop=False)
                return nc.tensor.matmul(dst, w_lo, m_hi, start=False, stop=stop)

            def xT(t, par):
                pe.wait_ge(x_in[par], arrivals(t, par, 16 * NSEG))
                if not isinstance(t, int) or t > 0:
                    pe.wait_ge(logit_read, t)
                for b in range(NB):
                    last = nc.tensor.transpose(psL0[:, b * L:(b + 1) * L], x_tok[:, par, b, :], ident[:, :])
                last.then_inc(xT_ps, 1)

            def low_rank_in(t):
                pe.wait_ge(F_lo_ok, t + 1)
                pe.wait_ge(xT_lo_ok, t + 1)
                product3(psZ, F_hi[:, :], F_lo[:, :], xT_hi[:, :], xT_lo[:, :], True, True).then_inc(z_ps, 1)

            def fT(t, par):
                nc.tensor.transpose(psFT, F_raw[:, par, :], ident[:, :]).then_inc(fT_ps, 1)

            def layer0(t):
                pe.wait_ge(z1_ok, t + 1)
                product3(psL0, WT_hi[:, :], WT_lo[:, :], xT_hi[:, :], xT_lo[:, :], True, False)
                pe.wait_ge(fT_lo_ok, 2 * t + 2)
                pe.wait_ge(z1_lo_ok, t + 1)
                product3(psL0, fT_hi[:, :], fT_lo[:, :], z1_hi[:, :], z1_lo[:, :], False, True).then_inc(y0_ps, 1)

            def gate_sum(t):
                pe.wait_ge(gate_fold_ok, t + 1)
                nc.tensor.matmul(psLogit, ones[:, :], gate_fold[:, :, :], start=True, stop=True).then_inc(logit_ps, 1)

            def up(t, par, s):
                k = NS * t + s
                if not isinstance(t, int) or t == 0:
                    wait_weight_lo(pe, 2 * s)
                if s == 0:
                    pe.wait_ge(x1_lo_ok, t + 1)
                for c in range(CH):
                    n = CH * k + c
                    if not isinstance(n, int) or n >= UP:
                        pe.wait_ge(h_ok, n - UP + 1)
                    product3(up_bank(s, c), W1_hi[:, s, c, :], W1_lo[:, s, c, :],
                             span(x1_hi[:, par, :], s), span(x1_lo[:, par, :], s), True, True).then_inc(up_ps, 1)

            def down(t, par, s):
                hf = half(par, s)
                if not isinstance(t, int):
                    wait_weight_lo(pe, 2 * s + 1)
                for c in range(CH):
                    if s == 0:
                        pe.wait_ge(shared_lo_ok, CH * t + c + 1)
                    elif c == 0:
                        pe.wait_ge(lo_ok, NB * (E * t + s))
                    last = product3(span(psY, s), W2_hi[:, s, c, :], W2_lo[:, s, c, :],
                                    span(hs_hi[:, hf, c, :], s), span(hs_lo[:, hf, c, :], s),
                                    s == 0 and c == 0, s == NS - 1 and c == CH - 1)
                if s == NS - 1:
                    last.then_inc(down_ok, 1)

            def tile(t, par, last=False):
                if not last:
                    xT(t + 1, 1 - par)
                down(t, par, 0)
                up(t, par, 2)
                if not last:
                    low_rank_in(t + 1)
                    fT(t + 1, 1 - par)
                down(t, par, 1)
                up(t, par, 3)
                if not last:
                    layer0(t + 1)
                down(t, par, 2)
                up(t, par, 4)
                down(t, par, 3)
                if not last:
                    up(t + 1, 1 - par, 0)
                    gate_sum(t + 1)
                down(t, par, 4)
                if not last:
                    up(t + 1, 1 - par, 1)
                pe.wait_ge(outT_ok, t + 1)
                for b in range(NB):
                    tr = nc.tensor.transpose(psOut[:, b * D:(b + 1) * D], outT[:, b * L:(b + 1) * L], ident[:, :])
                tr.then_inc(out_ps, 1)

            pe.wait_ge(ident_ok, 1)
            pe.wait_ge(W_in, 16)
            nc.tensor.transpose(psWT, W_raw[:, :], ident[:, :]).then_inc(WT_ps, 1)
            xT(0, 0)
            low_rank_in(0)
            fT(0, 0)
            pe.wait_ge(cond_in, 16)
            nc.tensor.transpose(psCondT, cond_raw[:, :], ident[0:B, 0:B]).then_inc(condT_ps, 1)
            pe.wait_ge(WT_lo_ok, 1)
            pe.wait_ge(zbias_ok, 2)
            layer0(0)
            pe.wait_ge(silu_ok, 1)
            up(0, 0, 0)
            pe.wait_ge(small_in, 16 * 6)
            nc.tensor.transpose(psEb2T, eb2_raw[:, :], ident[0:E, 0:E]).then_inc(eb2T_ps, 1)
            pe.wait_ge(ones_ok, 1)
            pe.wait_ge(mod_terms_ok, 1)
            nc.tensor.matmul(psMod, ones[:, :], mod_terms[:, :, :], start=True, stop=True).then_inc(mod_ps, 1)
            gate_sum(0)
            up(0, 0, 1)
            pe.wait_ge(mod_read, 1)
            pe.wait_ge(eb2T_read, 3)
            with pe.Fori(0, NT - 3, 2) as t:
                tile(t, 0)
                tile(t + 1, 1)
            tile(NT - 2, 0)
            tile(NT - 1, 1, last=True)

        @block.vector
        def _(dve):
            n_setup = 0

            def chained(ins):
                nonlocal n_setup
                n_setup += 1
                ins.then_inc(setup_step, 1)
                dve.wait_ge(setup_step, n_setup)

            def F_split(t, par):
                dve.wait_ge(F_in[par], arrivals(t, par, 16))
                nc.vector.tensor_copy(F_hi[:, :], F_raw[:, par, :]).then_inc(F_hi_ok, 1)
                dve.wait_ge(F_hi_ok, t + 1)
                nc.vector.tensor_tensor(F_lo[:, :], F_raw[:, par, :], f32(F_hi[:, :]), ALU.subtract
                                        ).then_inc(F_lo_ok, 1)

            def z1_mask(t):
                dve.wait_ge(z_ps, t + 1)
                nc.vector.tensor_tensor(z1[:, :], psZ, zmask[0:ZR, :, :].rearrange("p b l -> p (b l)"),
                                        ALU.mult).then_inc(z1_ok, 1)

            def fT_low(t, par):
                dve.wait_ge(fT_hi_ok, t + 1)
                nc.vector.tensor_tensor(fT_lo[ZR:KR, :], cond_rows[ZR:KR, par, :], f32(fT_hi[ZR:KR, :]),
                                        ALU.subtract).then_inc(fT_lo_ok, 1)
                nc.vector.tensor_tensor(fT_lo[0:ZR, :], psFT, f32(fT_hi[0:ZR, :]), ALU.subtract
                                        ).then_inc(fT_lo_ok, 1)

            def residual0(t, par):
                dve.wait_ge(g0_ok, t + 1)
                xs = x1[:, par, :]
                nc.vector.tensor_tensor(xs, xs, g0[:, :], ALU.add).then_inc(x1_ok, 1)
                dve.wait_ge(x1_ok, t + 1)
                nc.vector.tensor_copy(x1_hi[:, par, :], xs).then_inc(x1_hi_ok, 1)
                dve.wait_ge(x1_hi_ok, t + 1)
                nc.vector.tensor_tensor(x1_lo[:, par, :], xs, f32(x1_hi[:, par, :]), ALU.subtract
                                        ).then_inc(x1_lo_ok, 1)

            def gate_in(t, par):
                x1v = x1[:, par, :].rearrange("p (b l) -> p b l", l=L)
                for i, (at, _, n) in enumerate(SEGS):
                    nc.vector.tensor_reduce(segsum[:, i, :], x1v[:, :, at:at + n], AX.X, ALU.add
                                            ).then_inc(segsum_ok, 1)
                dve.wait_ge(segsum_ok, NSEG * t + NSEG)
                nc.vector.tensor_tensor(gate_terms[:, :, :, :],
                                        segsum[:, :, :].unsqueeze(3).to_broadcast([128, NSEG, NB, E]),
                                        gw[:, :, :].unsqueeze(2).to_broadcast([128, NSEG, NB, E]),
                                        ALU.mult).then_inc(gate_terms_ok, 1)
                dve.wait_ge(gate_terms_ok, t + 1)
                nc.vector.tensor_reduce(gate_fold[:, :, :], gate_terms[:, :, :, :].rearrange("p s b e -> p b e s"),
                                        AX.X, ALU.add).then_inc(gate_fold_ok, 1)

            def linked(ins, t, n):
                ins.then_inc(gate_step, 1)
                dve.wait_ge(gate_step, GATE_LINKS * t + n)

            def gate_logits(t):
                dve.wait_ge(logit_ps, t + 1)
                nc.vector.tensor_tensor(logit[:, :, :], psLogit, gate_mul[:, bass.ds(t * NB, NB), :],
                                        ALU.mult).then_inc(logit_read, 1)
                dve.wait_ge(logit_read, t + 1)
                linked(nc.vector.tensor_tensor(logit[:, :, :], logit[:, :, :], gate_add[:, bass.ds(t * NB, NB), :],
                                               ALU.add), t, 1)
                linked(nc.vector.tensor_reduce(top[:, :], logit[:, :, :], AX.X, ALU.max), t, 2)
                nc.vector.tensor_tensor(logit_x[:, :, :], logit[:, :, :],
                                        top[:, :].unsqueeze(2).to_broadcast([128, NB, E]),
                                        ALU.subtract).then_inc(logit_x_ok, 1)
                logit_e = logit[:, :, :].unsqueeze(3).to_broadcast([128, NB, E, E])
                logit_j = logit[:, :, :].unsqueeze(2).to_broadcast([128, NB, E, E])
                linked(nc.vector.tensor_tensor(equal[:, :, :, :], logit_j, logit_e, ALU.is_equal), t, 3)
                nc.vector.tensor_tensor(greater[:, :, :, :], logit_j, logit_e, ALU.is_gt)
                linked(nc.vector.tensor_tensor(equal[:, :, :, :], equal[:, :, :, :], before[:, :, :, :], ALU.mult), t, 4)
                linked(nc.vector.tensor_tensor(greater[:, :, :, :], greater[:, :, :, :], equal[:, :, :, :], ALU.add), t, 5)

            def gate_weights(t):
                dve.wait_ge(tanh_g_ok, t + 1)
                nc.vector.tensor_reduce(rank[:, :, :], greater[:, :, :, :], AX.X, ALU.add)
                linked(nc.vector.tensor_scalar(denom[:, :, :], tanh_g[:, :, :], -1.0, 1.0, ALU.mult, ALU.add), t, 6)
                nc.vector.tensor_scalar(numer[:, :, :], tanh_g[:, :, :], 1.0, None, ALU.add)
                linked(nc.vector.reciprocal(denom[:, :, :], denom[:, :, :]), t, 7)
                nc.vector.tensor_scalar(chosen[:, :, :], rank[:, :, :], 1.5, None, ALU.is_lt)
                linked(nc.vector.tensor_tensor(expd[:, :, :], numer[:, :, :], denom[:, :, :], ALU.mult), t, 8)
                nc.vector.tensor_reduce(sum_all[:, :], expd[:, :, :], AX.X, ALU.add)
                linked(nc.vector.tensor_tensor(exp_top[:, :, :], expd[:, :, :], chosen[:, :, :], ALU.mult), t, 9)
                linked(nc.vector.tensor_reduce(sum_top[:, :], exp_top[:, :, :], AX.X, ALU.add), t, 10)
                linked(nc.vector.scalar_tensor_tensor(sum_top[:, :], sum_all[:, :], 1e-8, sum_top[:, :],
                                                      ALU.mult, ALU.add), t, 11)
                linked(nc.vector.reciprocal(sum_top[:, :], sum_top[:, :]), t, 12)
                nc.vector.tensor_tensor(w_be[:, :, :], exp_top[:, :, :],
                                        sum_top[:, :].unsqueeze(2).to_broadcast([128, NB, E]),
                                        ALU.mult).then_inc(w_ok, 1)
                dve.wait_ge(w_ok, t + 1)
                for i in range(NSEG):
                    ins = nc.vector.tensor_tensor(bias_terms[:, i, :, :], w_be[:, :, :],
                                                  eb2T[:, i, :].unsqueeze(1).to_broadcast([128, NB, E]), ALU.mult)
                linked(ins, t, 13)
                linked(nc.vector.tensor_reduce(bias2[:, :, :], bias_terms[:, :, :, :], AX.X, ALU.add), t, 14)
                nc.vector.tensor_scalar(bias2[:, :, :], bias2[:, :, :], sb2_col[:, 0:1], None, ALU.add
                                        ).then_inc(bias2_ok, 1)

            def split(t, par, s):
                hf = half(par, s)
                a, z = SPAN[s]
                dve.wait_ge(h_ok, CH * (NS * t + s + 1))
                for b in range(NB if s < E else 0):
                    c = slice(b * L + a, b * L + z)
                    nc.vector.tensor_scalar(hs_hi[:, hf, :, c], h[:, hf, :, c], w_be[:, b, s - 1:s], None,
                                            ALU.mult).then_inc(hi_ok, 1)
                for b in range(NB):
                    c = slice(b * L + a, b * L + z)
                    if s < E:
                        dve.wait_ge(hi_ok, NB * ((E - 1) * t + s - 1) + b + 1)
                    else:
                        dve.wait_ge(hi4_ok, NB * t + b + 1)
                    nc.vector.scalar_tensor_tensor(hs_lo[:, hf, :, c], h[:, hf, :, c], w_be[:, b, s - 1:s],
                                                   f32(hs_hi[:, hf, :, c]), ALU.mult, ALU.subtract
                                                   ).then_inc(lo_ok, 1)

            def tile(t, par, last=False):
                if not last:
                    F_split(t + 1, 1 - par)
                split(t, par, 1)
                if not last:
                    z1_mask(t + 1)
                split(t, par, 2)
                if not last:
                    fT_low(t + 1, 1 - par)
                split(t, par, 3)
                if not last:
                    residual0(t + 1, 1 - par)
                    gate_in(t + 1, 1 - par)
                split(t, par, 4)
                dve.wait_ge(x1b_ok, NSEG * (t + 1))
                if not last:
                    gate_logits(t + 1)
                dve.wait_ge(down_ok, t + 1)
                nc.vector.tensor_tensor(outT[:, :], psY, x1[:, par, :], ALU.add).then_inc(outT_ok, 1)
                if not last:
                    gate_weights(t + 1)

            dve.wait_ge(zmask_ok, 1)
            nc.vector.tensor_copy(z1_hi[ZR:KR, :], zmask[ZR:KR, :, :].rearrange("p b l -> p (b l)")
                                  ).then_inc(zbias_ok, 1)
            nc.vector.memset(f32(z1_lo[ZR:KR, :]), 0.0).then_inc(zbias_ok, 1)
            F_split(0, 0)
            dve.wait_ge(x_fp_ok, 1)
            dve.wait_ge(xT_hi_ok, 1)
            nc.vector.tensor_tensor(xT_lo[:, :], x1[:, 0, :], f32(xT_hi[:, :]), ALU.subtract).then_inc(xT_lo_ok, 1)
            dve.wait_ge(WT_hi_ok, 1)
            nc.vector.tensor_tensor(WT_lo[:, :], psWT, f32(WT_hi[:, :]), ALU.subtract).then_inc(WT_lo_ok, 1)
            fT_low(0, 0)
            z1_mask(0)
            make_weight_lo(dve, 0)
            dve.wait_ge(z1_hi_ok, 1)
            nc.vector.tensor_tensor(z1_lo[0:ZR, :], z1[:, :], f32(z1_hi[0:ZR, :]), ALU.subtract
                                    ).then_inc(z1_lo_ok, 1)
            make_weight_lo(dve, 2)
            dve.wait_ge(small_in, 16 * 6)
            inv = 1.0 / (HEAD + PROP)
            chained(nc.vector.tensor_scalar(gw_full[:, :], gate_raw[:, 0, :], 1.0 / L, None, ALU.mult))
            chained(nc.vector.scalar_tensor_tensor(gw[:, 0, :], gate_raw[:, 1, :], inv, gw_full[:, :],
                                                   ALU.mult, ALU.add))
            nc.vector.scalar_tensor_tensor(gw[:, 2, :], gate_raw[:, 2, :], inv, gw_full[:, :], ALU.mult, ALU.add)
            chained(nc.vector.scalar_tensor_tensor(gw[:, 1, :], gate_raw[:, 2, :], inv, gw[:, 0, :],
                                                   ALU.mult, ALU.add))
            chained(nc.vector.tensor_scalar(tw[:, :], time_w_raw[:, :], 0.5, None, ALU.mult))
            dve.wait_ge(tanh_c_ok, 1)
            nc.vector.scalar_tensor_tensor(silu2[:, :], tanh_c[:, :], 1.0, psCondT, ALU.add, ALU.mult
                                           ).then_inc(silu_ok, 1)
            dve.wait_ge(silu_ok, 1)
            nc.vector.tensor_tensor(mod_terms[:, :, :], silu2[:, :].unsqueeze(2).to_broadcast([128, B, 2 * E]),
                                    tw[:, :].unsqueeze(1).to_broadcast([128, B, 2 * E]), ALU.mult
                                    ).then_inc(mod_terms_ok, 1)
            residual0(0, 0)
            gate_in(0, 0)
            make_weight_lo(dve, 4)
            dve.wait_ge(eb2T_ps, 1)
            for i in range(NSEG):
                nc.vector.tensor_copy(eb2T[:, i, :], psEb2T).then_inc(eb2T_read, 1)
            dve.wait_ge(eb2T_read, NSEG)
            nc.vector.memset(eb2T[:, 2, 1:2], 0.0)
            chained(nc.vector.memset(eb2T[:, 0, 2:3], 0.0))
            dve.wait_ge(mod_ps, 1)
            nc.vector.tensor_tensor(mod[:, :, :], psMod, time_b_row[:, :].unsqueeze(1).to_broadcast([128, B, 2 * E]),
                                    ALU.add).then_inc(mod_read, 1)
            dve.wait_ge(mod_read, 1)
            chained(nc.vector.tensor_scalar(gate_mul[:, :, :], mod[:, :, 0:E], 1.0, None, ALU.add))
            chained(nc.vector.tensor_tensor(gate_add[:, :, :], gate_mul[:, :, :],
                                            gate_b_row[:, :].unsqueeze(1).to_broadcast([128, B, E]), ALU.mult))
            chained(nc.vector.tensor_tensor(gate_add[:, :, :], gate_add[:, :, :], mod[:, :, E:2 * E], ALU.add))
            dve.wait_ge(before_ok, 1)
            gate_logits(0)
            gate_weights(0)
            make_weight_lo(dve, 6)
            make_weight_lo(dve, 8)
            with dve.Fori(0, NT - 3, 2) as t:
                tile(t, 0)
                tile(t + 1, 1)
            tile(NT - 2, 0)
            tile(NT - 1, 1, last=True)


_INS = ["x", "fside_Bx1x1024x16_0", "cond_1024", "L0_cond_W", "L0_cond_fc_bias", "L1_cond_gate_w", "L1_cond_gate_b",
        "L1_cond_time_w", "L1_cond_time_b", "L1_cond_ew1", "L1_cond_eb1", "L1_cond_ew2", "L1_cond_eb2",
        "L1_cond_sw1", "L1_cond_sb1", "L1_cond_sw2", "L1_cond_sb2"]


def kernel(**inputs):
    import numpy as np
    import concourse.bacc as bacc
    from concourse.bass_utils import run_bass_kernel_spmd

    nc = bacc.Bacc("TRN2", target_bir_lowering=False, num_devices=1)
    arrays, args = {}, []
    for name in _INS:
        a = np.ascontiguousarray(inputs[name])
        arrays[f"in_{name}"] = a
        args.append(nc.dram_tensor(f"in_{name}", a.shape, mybir.dt.from_np(a.dtype), kind="ExternalInput").ap())
    shape = arrays["in_x"].shape
    args.append(nc.dram_tensor("out_0", shape, F32, kind="ExternalOutput").ap())
    build(nc, *args)
    r = run_bass_kernel_spmd(nc, [arrays], core_ids=[0])
    return r.results[0]["out_0"]
```

```python
from contextlib import ExitStack

import concourse.bass as bass
from concourse import mybir

F32 = mybir.dt.float32
F32R = mybir.dt.float32r
ALU = mybir.AluOpType
ACT = mybir.ActivationFunctionType
AX = mybir.AxisListType


def build(nc, x, fside, cond, W, fc_bias, gate_w, gate_b, time_w, time_b,
          ew1, eb1, ew2, eb2, sw1, sb1, sw2, sb2, out):
    B, L, D = x.shape
    R = fside.shape[-1]
    E, _, H = ew1.shape
    NB = 4
    NT = B // NB
    TOK = NB * L
    CH = H // 128
    HEAD = L // 3
    PROP = L - 2 * HEAD
    SEGS = [(0, 0, HEAD), (HEAD, 2 * HEAD, PROP), (HEAD + PROP, HEAD, HEAD)]
    NSEG = len(SEGS)
    NS = E + 1
    SPAN = [(0, L), (0, L), (0, HEAD + PROP), (HEAD, L), (0, L)]
    Z_SCALE = 1.0 / (D * R)
    ZR = NB * R
    BIAS_HI, BIAS_LO = ZR, ZR + 32
    UP = 5
    BANK_Y, BANK_OUT, BANK_L0 = 5, 6, 7
    GATE_LINKS = 14

    with ExitStack() as ctx:
        def sb(name, shape, dt=F32):
            return ctx.enter_context(nc.sbuf_tensor(name, shape, dt))

        def sem(name):
            return ctx.enter_context(nc.semaphore(name))

        ps = ctx.enter_context(nc.psum_tensor("ps", [128, 8, 512], F32))

        x_tok = sb("x_tok", [128, 2, NB, D])
        F_raw = sb("F_raw", [128, 2, 2, ZR])
        W_raw = sb("W_raw", [128, D])
        cond_raw = sb("cond_raw", [B, D])
        cond_rows = sb("cond_rows", [128, 2, D])
        fcb = sb("fcb", [128, 1])
        sb2_col = sb("sb2_col", [128, 1])
        gate_raw = sb("gate_raw", [128, 3, E])
        gate_b_row = sb("gate_b_row", [128, E])
        time_w_raw = sb("time_w_raw", [128, 2 * E])
        time_b_row = sb("time_b_row", [128, 2 * E])
        eb2_raw = sb("eb2_raw", [E, D])
        b1_col = sb("b1_col", [128, NS, CH])
        W1_raw = sb("W1_raw", [128, NS, H])
        W2_raw = sb("W2_raw", [128, NS, H])
        ident = sb("ident", [128, 128])
        ones = sb("ones", [128, 128])
        batch_rows = sb("batch_rows", [128, NB])
        zmask_halves = sb("zmask_halves", [128, 2, NB])
        zmask = sb("zmask", [128, NB])
        before = sb("before", [128, NB, E, E])
        WT_hi = sb("WT_hi", [128, D], F32R)
        WT_lo = sb("WT_lo", [128, D], F32R)
        W1_hi = sb("W1_hi", [128, NS, CH, 128], F32R)
        W1_lo = sb("W1_lo", [128, NS, CH, 128], F32R)
        W2_hi = sb("W2_hi", [128, NS, CH, 128], F32R)
        W2_lo = sb("W2_lo", [128, NS, CH, 128], F32R)
        F_hi = sb("F_hi", [128, 2 * ZR], F32R)
        F_lo = sb("F_lo", [128, 2 * ZR], F32R)
        fT = sb("fT", [2 * ZR, D], F32R)
        fT_bias = sb("fT_bias", [128, D], F32R)
        xT_hi = sb("xT_hi", [128, TOK], F32R)
        xT_lo = sb("xT_lo", [128, TOK], F32R)
        z1 = sb("z1", [2 * ZR, TOK])
        z1_hi = sb("z1_hi", [2 * ZR, TOK], F32R)
        z1_lo = sb("z1_lo", [128, TOK], F32R)
        g0 = sb("g0", [128, TOK])
        x1 = sb("x1", [128, 2, TOK])
        x1_hi = sb("x1_hi", [128, 2, TOK], F32R)
        x1_lo = sb("x1_lo", [128, 2, TOK], F32R)
        tanh_c = sb("tanh_c", [128, B])
        silu2 = sb("silu2", [128, B])
        tw = sb("tw", [128, 2 * E])
        mod_terms = sb("mod_terms", [128, B, 2 * E])
        mod = sb("mod", [128, B, 2 * E])
        gate_mul = sb("gate_mul", [128, B, E])
        gate_add = sb("gate_add", [128, B, E])
        gw_full = sb("gw_full", [128, E])
        gw = sb("gw", [128, NSEG, E])
        eb2T = sb("eb2T", [128, NSEG, E])
        segsum = sb("segsum", [128, NSEG, NB])
        gate_terms = sb("gate_terms", [128, NSEG, NB, E])
        gate_fold = sb("gate_fold", [128, NB, E])
        logit = sb("logit", [128, NB, E])
        logit_x = sb("logit_x", [128, NB, E])
        top = sb("top", [128, NB])
        tanh_g = sb("tanh_g", [128, NB, E])
        numer = sb("numer", [128, NB, E])
        denom = sb("denom", [128, NB, E])
        expd = sb("expd", [128, NB, E])
        exp_top = sb("exp_top", [128, NB, E])
        greater = sb("greater", [128, NB, E, E])
        equal = sb("equal", [128, NB, E, E])
        rank = sb("rank", [128, NB, E])
        chosen = sb("chosen", [128, NB, E])
        sum_all = sb("sum_all", [128, NB])
        sum_top = sb("sum_top", [128, NB])
        w_be = sb("w_be", [128, NB, E])
        bias_terms = sb("bias_terms", [128, NSEG, NB, E])
        bias2 = sb("bias2", [128, NSEG, NB])
        h = sb("h", [128, 2, CH, TOK])
        hs_hi = sb("hs_hi", [128, 2, CH, TOK], F32R)
        hs_lo = sb("hs_lo", [128, 2, CH, TOK], F32R)
        outT = sb("outT", [128, TOK])
        out_tok = sb("out_tok", [128, NB, D])
        table_probe = sb("table_probe", [128, 3])

        x_in = [sem("x_in_even"), sem("x_in_odd")]
        F_in = [sem("F_in_even"), sem("F_in_odd")]
        rows_in = [sem("rows_in_even"), sem("rows_in_odd")]
        W_in, cond_in, fcb_in, gate_loads_in, bias_in, b1_in = (
            sem("W_in"), sem("cond_in"), sem("fcb_in"), sem("gate_loads_in"), sem("bias_in"), sem("b1_in"))
        w_in = [sem(f"w_in{n}") for n in range(2 * NS)]
        probe_ok, hi4_ok = sem("probe_ok"), sem("hi4_ok")
        const_step, ident_ok, ones_ok, zmask_ok, before_ok = (sem("const_step"), sem("ident_ok"), sem("ones_ok"),
                                                              sem("zmask_ok"), sem("before_ok"))
        batch_rows_ok, rows_zero_ok, z1_rows_ok = sem("batch_rows_ok"), sem("rows_zero_ok"), sem("z1_rows_ok")
        WT_ps, condT_ps, eb2T_ps, WT_hi_ok, WT_lo_ok = (sem("WT_ps"), sem("condT_ps"), sem("eb2T_ps"),
                                                        sem("WT_hi_ok"), sem("WT_lo_ok"))
        w_hi_ok = [sem(f"w_hi_ok{n}") for n in range(2 * NS)]
        w_lo_ok = [sem(f"w_lo_ok{n}") for n in range(2 * NS)]
        tanh_c_ok, setup_step, mod_terms_ok, mod_ps, mod_read, silu_ok, eb2T_read = (
            sem("tanh_c_ok"), sem("setup_step"), sem("mod_terms_ok"), sem("mod_ps"), sem("mod_read"),
            sem("silu_ok"), sem("eb2T_read"))
        xT_ps, x_fp_ok, xT_hi_ok, xT_lo_ok = sem("xT_ps"), sem("x_fp_ok"), sem("xT_hi_ok"), sem("xT_lo_ok")
        F_hi_ok, F_lo_ok, fT_ps, fT_hi_ok, fT_lo_ok = (sem("F_hi_ok"), sem("F_lo_ok"), sem("fT_ps"),
                                                       sem("fT_hi_ok"), sem("fT_lo_ok"))
        z_ps, z1_ok, z1_hi_ok, z1_lo_ok = sem("z_ps"), sem("z1_ok"), sem("z1_hi_ok"), sem("z1_lo_ok")
        y0_ps, g0_ok, x1_ok, x1_hi_ok, x1_lo_ok = (sem("y0_ps"), sem("g0_ok"), sem("x1_ok"), sem("x1_hi_ok"),
                                                   sem("x1_lo_ok"))
        gate_fold_ok = sem("gate_fold_ok")
        segsum_ok, gate_terms_ok, logit_ps, logit_read = (sem("segsum_ok"), sem("gate_terms_ok"), sem("logit_ps"),
                                                          sem("logit_read"))
        gate_step, logit_x_ok, tanh_g_ok, w_ok, bias2_ok, x1b_ok = (
            sem("gate_step"), sem("logit_x_ok"), sem("tanh_g_ok"), sem("w_ok"), sem("bias2_ok"), sem("x1b_ok"))
        up_ps, h_ok, shared_lo_ok, hi_ok, lo_ok, down_ok = (
            sem("up_ps"), sem("h_ok"), sem("shared_lo_ok"), sem("hi_ok"), sem("lo_ok"), sem("down_ok"))
        outT_ok, out_ps, out_tok_ok, out_left = sem("outT_ok"), sem("out_ps"), sem("out_tok_ok"), sem("out_left")

        psL0 = ps[:, BANK_L0, :]
        psZ = ps[:, BANK_L0, :]
        psLogit = ps[:, BANK_L0, 0:NB * E].rearrange("p (b e) -> p b e", e=E)
        psZ_first = ps[:, 2, :]
        psFT = ps[:, BANK_OUT, 0:D]
        psOut = ps[:, BANK_OUT, :]
        psY = ps[:, BANK_Y, :]
        HALF = NB // 2 * L
        psY_half = [ps[:, BANK_Y, 0:HALF], ps[:, BANK_L0, 0:HALF]]
        psOut_half = [ps[:, BANK_OUT, 0:HALF], ps[:, 0, 0:HALF]]
        psWT, psCondT, psEb2T = ps[:, 0, 0:D], ps[:, BANK_Y, E:E + B], ps[:, BANK_Y, 0:E]
        psIdle = ps[:, 4, 0:128]
        psMod = ps[:, BANK_OUT, 0:B * 2 * E].rearrange("p (b e) -> p b e", e=2 * E)

        block = ctx.enter_context(nc.Block())

        def f32(ap):
            return ap.bitcast(F32)

        def span(ap, s):
            a, z = SPAN[s]
            return ap if z - a == L else ap.rearrange("p (b l) -> p b l", l=L)[:, :, a:z]

        def half(par, s):
            return (NS * par + s) % 2

        def up_bank(s, c):
            a, z = SPAN[s]
            bank = ps[:, (s * CH + c) % UP, 0:NB * (z - a)]
            return bank if z - a == L else bank.rearrange("p (b l) -> p b l", b=NB)

        def arrivals(t, par, each):
            return (t - par) * (each // 2) + each

        def weight(n):
            e = n // 2
            if n % 2 == 0:
                return W1_raw[:, e, :].rearrange("p (m c) -> p c m", c=CH), W1_hi[:, e, :, :], W1_lo[:, e, :, :]
            return W2_raw[:, e, :].rearrange("p (c m) -> p c m", c=CH), W2_hi[:, e, :, :], W2_lo[:, e, :, :]

        def wait_weight_lo(eng, n):
            eng.wait_ge(w_lo_ok[n], 1)

        def make_weight_hi(eng, n):
            eng.wait_ge(w_in[n], 16)
            raw, hi, _ = weight(n)
            eng.tensor_copy(hi, raw).then_inc(w_hi_ok[n], 1)

        def make_weight_lo(eng, n):
            eng.wait_ge(w_hi_ok[n], 1)
            raw, hi, lo = weight(n)
            eng.tensor_tensor(lo, raw, f32(hi), ALU.subtract).then_inc(w_lo_ok[n], 1)

        @block.sync
        def _(sp):
            def load(t, par, segs=SEGS, copies=(0, 1)):
                b = t * NB
                for at, src, n in segs:
                    sp.dma_start(x_tok[at:at + n, par, :, :],
                                 x[bass.ds(b, NB), src:src + n, :].rearrange("b l d -> l b d")
                                 ).then_inc(x_in[par], 16)
                for copy in copies:
                    sp.dma_start(F_raw[:, par, copy, :].rearrange("i (b r) -> i b r", r=R),
                                 fside[bass.ds(b, NB), 0, :, :].rearrange("b i r -> i b r")).then_inc(F_in[par], 16)
                sp.wait_ge(rows_zero_ok, 1)
                for row in (BIAS_HI, BIAS_LO):
                    sp.dma_start(cond_rows[row:row + NB, par, :], cond[bass.ds(b, NB), :]).then_inc(rows_in[par], 16)

            def store(t):
                sp.wait_ge(out_tok_ok, t + 1)
                sp.dma_start(out[bass.ds(t * NB, NB), :, :].rearrange("b l d -> l b d"), out_tok[:, :, :]
                             ).then_inc(out_left, 16)

            def tile(t, par):
                sp.wait_ge(xT_ps, t + 1)
                sp.wait_ge(F_lo_ok, t + 1)
                sp.wait_ge(fT_lo_ok, 2 * t + 2)
                load(t + 2, par)
                store(t)

            def load_weight(n):
                e = n // 2
                if n % 2 == 0:
                    sp.dma_start(W1_raw[:, e, :], sw1 if e == 0 else ew1[e - 1]).then_inc(w_in[n], 16)
                else:
                    src = sw2 if e == 0 else ew2[e - 1]
                    sp.dma_start(W2_raw[:, e, :], src.rearrange("(p c) d -> p (c d)", c=CH)).then_inc(w_in[n], 16)

            load(0, 0, SEGS[::2], (0,))
            for n in (0, 2, 1, 3, 4):
                load_weight(n)
            sp.dma_start(b1_col[:, 0, :], sb1.rearrange("(p c) -> p c", c=CH)).then_inc(b1_in, 16)
            sp.dma_start(b1_col[:, 1:NS, :], eb1.rearrange("e (p c) -> p e c", c=CH)).then_inc(b1_in, 16)
            for dst, src in (
                    (gate_raw[:, :, :], gate_w.rearrange("(g d) e -> d g e", g=3)),
                    (gate_b_row[:, :], gate_b.rearrange("(a e) -> a e", a=1).to_broadcast([128, E])),
                    (time_w_raw[:, :], time_w)):
                sp.dma_start(dst, src).then_inc(gate_loads_in, 16)
            for n in (6, 5, 8, 7, 9):
                load_weight(n)
            load(1, 1)
            with sp.Fori(0, NT - 3, 2) as t:
                tile(t, 0)
                tile(t + 1, 1)
            store(NT - 2)
            for g in range(2):
                sp.wait_ge(out_tok_ok, NT + g)
                b = (NT - 1) * NB + g * NB // 2
                sp.dma_start(out[b:b + NB // 2, :, :].rearrange("b l d -> l b d"),
                             out_tok[:, g * NB // 2:(g + 1) * NB // 2, :]).then_inc(out_left, 16)
            sp.wait_ge(out_left, 16 + 16 * (NT + 1))

        @block.gpsimd
        def _(pool):
            n_const = 0

            def chained(ins):
                nonlocal n_const
                n_const += 1
                ins.then_inc(const_step, 1)
                pool.wait_ge(const_step, n_const)

            nc.gpsimd.memset(ones[:, :], 1.0).then_inc(ones_ok, 1)
            nc.gpsimd.memset(table_probe[:, :], 0.0).then_inc(probe_ok, 1)
            chained(nc.gpsimd.memset(ident[:, :], 0.0))
            nc.gpsimd.affine_select(out=ident[:, :], in_=ident[:, :], compare_op=ALU.not_equal, fill=1.0, base=0,
                                    pattern=[[-1, 128]], channel_multiplier=1).then_inc(ident_ok, 1)
            chained(nc.gpsimd.memset(zmask_halves[:, :, :], Z_SCALE))
            chained(nc.gpsimd.affine_select(out=zmask_halves[:, :, :], in_=zmask_halves[:, :, :],
                                            compare_op=ALU.is_ge, fill=0.0, base=0,
                                            pattern=[[-ZR, 2], [-R, NB]], channel_multiplier=1))
            chained(nc.gpsimd.affine_select(out=zmask_halves[:, :, :], in_=zmask_halves[:, :, :],
                                            compare_op=ALU.is_ge, fill=0.0, base=R - 1,
                                            pattern=[[ZR, 2], [R, NB]], channel_multiplier=-1))
            nc.gpsimd.tensor_tensor(zmask[:, :], zmask_halves[:, 0, :], zmask_halves[:, 1, :], ALU.add
                                    ).then_inc(zmask_ok, 1)
            pool.dma_start(cond_raw[:, :], cond).then_inc(cond_in, 16)
            pool.dma_start(fcb[:, :], fc_bias.rearrange("(p a) -> p a", a=1)).then_inc(fcb_in, 16)
            chained(nc.gpsimd.memset(batch_rows[:, :], 0.0))
            chained(nc.gpsimd.affine_select(out=batch_rows[:, :], in_=batch_rows[:, :], compare_op=ALU.not_equal,
                                            fill=1.0, base=-BIAS_HI, pattern=[[-1, NB]], channel_multiplier=1))
            nc.gpsimd.affine_select(out=batch_rows[:, :], in_=batch_rows[:, :], compare_op=ALU.not_equal,
                                    fill=1.0, base=-BIAS_LO, pattern=[[-1, NB]], channel_multiplier=1
                                    ).then_inc(batch_rows_ok, 1)
            chained(nc.gpsimd.memset(before[:, :, :, :], 1.0))
            nc.gpsimd.affine_select(out=before[:, :, :, :], in_=before[:, :, :, :], compare_op=ALU.is_ge, fill=0.0,
                                    base=-1, pattern=[[0, NB], [1, E], [-1, E]], channel_multiplier=0
                                    ).then_inc(before_ok, 1)

            def xT_low(t, par):
                pool.wait_ge(x_fp_ok, t + 1)
                pool.wait_ge(xT_hi_ok, t + 1)
                nc.gpsimd.tensor_tensor(xT_lo[:, :], x1[:, par, :], f32(xT_hi[:, :]), ALU.subtract
                                        ).then_inc(xT_lo_ok, 1)

            def z1_low(t):
                pool.wait_ge(z1_hi_ok, t + 1)
                nc.gpsimd.tensor_tensor(z1_lo[0:ZR, :], z1[0:ZR, :], f32(z1_hi[0:ZR, :]), ALU.subtract
                                        ).then_inc(z1_lo_ok, 1)

            def output_bias(t, par):
                pool.wait_ge(bias2_ok, t + 1)
                xb = x1[:, par, :].rearrange("p (b l) -> p b l", l=L)
                for i, (at, _, n) in enumerate(SEGS):
                    nc.gpsimd.tensor_tensor(xb[:, :, at:at + n], xb[:, :, at:at + n],
                                            bias2[:, i, :].unsqueeze(2).to_broadcast([128, NB, n]),
                                            ALU.add).then_inc(x1b_ok, 1)

            def shared_low(t, par):
                k = NS * t
                for c in range(CH):
                    pool.wait_ge(h_ok, CH * k + c + 1)
                    hf = half(par, 0)
                    nc.gpsimd.tensor_tensor(hs_lo[:, hf, c, :], h[:, hf, c, :], f32(hs_hi[:, hf, c, :]),
                                            ALU.subtract).then_inc(shared_lo_ok, 1)

            def tile(t, par, last=False):
                if not last:
                    xT_low(t + 1, 1 - par)
                    z1_low(t + 1)
                output_bias(t, par)
                if not last:
                    shared_low(t + 1, 1 - par)

            for dst, src in (
                    (time_b_row[:, :], time_b.rearrange("(a e) -> a e", a=1).to_broadcast([128, 2 * E])),
                    (eb2_raw[:, :], eb2),
                    (sb2_col[:, :], sb2.rearrange("(p a) -> p a", a=1))):
                pool.dma_start(dst, src).then_inc(bias_in, 16)
            make_weight_lo(pool, 1)
            make_weight_lo(pool, 3)
            make_weight_lo(pool, 4)
            make_weight_lo(pool, 5)
            shared_low(0, 0)
            make_weight_lo(pool, 7)
            make_weight_lo(pool, 8)
            make_weight_lo(pool, 9)
            with pool.Fori(0, NT - 3, 2) as t:
                tile(t, 0)
                tile(t + 1, 1)
            tile(NT - 2, 0)
            tile(NT - 1, 1, last=True)

        @block.scalar
        def _(act):
            act.sem_inc(out_left, 16)
            at, src, n = SEGS[1]
            act.dma_start(x_tok[at:at + n, 0, :, :], x[0:NB, src:src + n, :].rearrange("b l d -> l b d")
                          ).then_inc(x_in[0], 16)
            act.dma_start(F_raw[:, 0, 1, :].rearrange("i (b r) -> i b r", r=R),
                          fside[0:NB, 0, :, :].rearrange("b i r -> i b r")).then_inc(F_in[0], 16)
            act.dma_start(W_raw[:, :], W).then_inc(W_in, 16)

            def weight_high(n):
                act.wait_ge(w_in[n], 16)
                raw, hi, _ = weight(n)
                nc.scalar.activation(hi, raw, ACT.Copy).then_inc(w_hi_ok[n], 1)

            def xT_copies(t, par):
                act.wait_ge(xT_ps, t + 1)
                nc.scalar.activation(x1[:, par, :], psL0, ACT.Copy).then_inc(x_fp_ok, 1)
                nc.scalar.activation(xT_hi[:, :], psL0, ACT.Copy).then_inc(xT_hi_ok, 1)

            def fT_high(t, par):
                act.wait_ge(rows_in[par], arrivals(t, par, 32))
                nc.scalar.activation(fT_bias[BIAS_HI:128, :], cond_rows[BIAS_HI:128, par, :], ACT.Copy)
                act.wait_ge(fT_ps, t + 1)
                nc.scalar.activation(fT_bias[0:ZR, :], psFT[0:ZR, :], ACT.Copy)
                nc.scalar.activation(fT[:, :], psFT, ACT.Copy).then_inc(fT_hi_ok, 1)

            def z1_high(t):
                act.wait_ge(z1_ok, t + 1)
                nc.scalar.activation(z1_hi[:, :], z1[:, :], ACT.Copy).then_inc(z1_hi_ok, 1)

            def gelu0(t):
                act.wait_ge(y0_ps, t + 1)
                nc.scalar.activation(g0[:, :], psL0, ACT.Gelu, bias=fcb[:, 0:1]).then_inc(g0_ok, 1)

            def preload_gelu(t):
                act.wait_ge(probe_ok, t + 1)
                nc.scalar.activation(table_probe[:, 1:2], table_probe[:, 0:1], ACT.Gelu).then_inc(probe_ok, 1)

            def expert4_high(t, par, first=0):
                act.wait_ge(w_ok, t + 1)
                act.wait_ge(h_ok, CH * (NS * t + NS))
                for b in range(first, NB):
                    c = slice(b * L, (b + 1) * L)
                    hf = half(par, NS - 1)
                    nc.scalar.activation(hs_hi[:, hf, :, c], h[:, hf, :, c], ACT.Copy, scale=w_be[:, b, E - 1:E]
                                         ).then_inc(hi4_ok, 1)

            def gate_tanh(t):
                act.wait_ge(logit_x_ok, t + 1)
                nc.scalar.activation(tanh_g[:, :, :], logit_x[:, :, :], ACT.Tanh, scale=0.5).then_inc(tanh_g_ok, 1)

            def gelu(t, par, s):
                k = NS * t + s
                for c in range(CH):
                    act.wait_ge(up_ps, CH * k + c + 1)
                    hf = half(par, s)
                    dst = span(h[:, hf, c, :], s)
                    ins = nc.scalar.activation(dst, up_bank(s, c), ACT.Gelu_apprx_tanh, bias=b1_col[:, s, c:c + 1])
                    if s == 0:
                        ins = nc.scalar.activation(hs_hi[:, hf, c, :], up_bank(s, c), ACT.Gelu_apprx_tanh,
                                                   bias=b1_col[:, s, c:c + 1])
                    ins.then_inc(h_ok, 1)

            def tile(t, par, last=False):
                if not last:
                    xT_copies(t + 1, 1 - par)
                gelu(t, par, 2)
                if not last:
                    fT_high(t + 1, 1 - par)
                    z1_high(t + 1)
                gelu(t, par, 3)
                if not last:
                    preload_gelu(t + 1)
                    gelu0(t + 1)
                gelu(t, par, 4)
                expert4_high(t, par, 1 if last else 0)
                if not last:
                    gelu(t + 1, 1 - par, 0)
                    gate_tanh(t + 1)
                    gelu(t + 1, 1 - par, 1)
                if last:
                    act.wait_ge(out_left, 16 * t + 16)
                    for g in range(2):
                        act.wait_ge(out_ps, t + g + 1)
                        nc.scalar.activation(out_tok[:, g * NB // 2:(g + 1) * NB // 2, :],
                                             psOut_half[g].rearrange("p (b d) -> p b d", d=D),
                                             ACT.Copy).then_inc(out_tok_ok, 1)
                    return
                act.wait_ge(out_ps, t + 1)
                act.wait_ge(out_left, 16 * t + 16)
                nc.scalar.activation(out_tok[:, :, :], psOut.rearrange("p (b d) -> p b d", d=D),
                                     ACT.Copy).then_inc(out_tok_ok, 1)

            preload_gelu(0)
            act.wait_ge(xT_ps, 1)
            nc.scalar.activation(xT_hi[:, :], psL0, ACT.Copy).then_inc(xT_hi_ok, 1)
            act.wait_ge(WT_ps, 1)
            nc.scalar.activation(WT_hi[:, :], psWT, ACT.Copy).then_inc(WT_hi_ok, 1)
            act.wait_ge(xT_lo_ok, 1)
            nc.scalar.activation(x1[:, 0, :], psL0, ACT.Copy).then_inc(x_fp_ok, 1)
            fT_high(0, 0)
            z1_high(0)
            for n in (0, 2, 3):
                weight_high(n)
            act.wait_ge(fcb_in, 16)
            gelu0(0)
            nc.scalar.activation(table_probe[:, 2:3], table_probe[:, 0:1], ACT.Gelu_apprx_tanh)
            act.wait_ge(condT_ps, 1)
            nc.scalar.activation(tanh_c[:, :], psCondT, ACT.Tanh, scale=0.5).then_inc(tanh_c_ok, 1)
            for n in (5, 6):
                weight_high(n)
            act.wait_ge(b1_in, 32)
            gelu(0, 0, 0)
            weight_high(7)
            gate_tanh(0)
            weight_high(8)
            gelu(0, 0, 1)
            weight_high(9)
            with act.Fori(0, NT - 3, 2) as t:
                tile(t, 0)
                tile(t + 1, 1)
            tile(NT - 2, 0)
            tile(NT - 1, 1, last=True)

        @block.tensor
        def _(pe):
            def product_hi(dst, w_hi, w_lo, m_hi, start):
                nc.tensor.matmul(dst, w_hi, m_hi, start=start, stop=False)
                nc.tensor.matmul(dst, w_lo, m_hi, start=False, stop=False)

            def product_lo(dst, w_hi, m_lo, stop):
                return nc.tensor.matmul(dst, w_hi, m_lo, start=False, stop=stop)

            def product3(dst, w_hi, w_lo, m_hi, m_lo, start, stop):
                product_hi(dst, w_hi, w_lo, m_hi, start)
                return product_lo(dst, w_hi, m_lo, stop)

            def keep_busy(n, dst=psIdle):
                for _ in range(n):
                    nc.tensor.matmul(dst, ones[:, :], ones[:, :], start=True, stop=True)

            def xT(t, par):
                pe.wait_ge(x_in[par], arrivals(t, par, 16 * NSEG))
                if not isinstance(t, int) or t > 0:
                    pe.wait_ge(logit_read, t)
                for b in range(NB):
                    last = nc.tensor.transpose(psL0[:, b * L:(b + 1) * L], x_tok[:, par, b, :], ident[:, :])
                last.then_inc(xT_ps, 1)

            def low_rank_in(t):
                first = isinstance(t, int) and t == 0
                dst = psZ_first if first else psZ
                pe.wait_ge(F_lo_ok, t + 1)
                if first:
                    pe.wait_ge(xT_hi_ok, t + 1)
                else:
                    pe.wait_ge(xT_lo_ok, t + 1)
                product_hi(dst, F_hi[:, :], F_lo[:, :], xT_hi[:, :], True)
                if first:
                    pe.wait_ge(xT_lo_ok, t + 1)
                product_lo(dst, F_hi[:, :], xT_lo[:, :], True).then_inc(z_ps, 1)

            def transpose_F(t, par):
                nc.tensor.transpose(psFT, F_raw[:, par, :, :].rearrange("i c r -> i (c r)"), ident[:, :]
                                    ).then_inc(fT_ps, 1)

            def layer0(t):
                if isinstance(t, int) and t == 0:
                    pe.wait_ge(x_fp_ok, 1)
                else:
                    pe.wait_ge(z1_ok, t + 1)
                product3(psL0, WT_hi[:, :], WT_lo[:, :], xT_hi[:, :], xT_lo[:, :], True, False)
                if isinstance(t, int) and t == 0:
                    keep_busy(2)
                pe.wait_ge(fT_lo_ok, 2 * t + 2)
                pe.wait_ge(z1_hi_ok, t + 1)
                nc.tensor.matmul(psL0, fT[:, :], z1_hi[:, :], start=False, stop=False)
                pe.wait_ge(z1_lo_ok, t + 1)
                nc.tensor.matmul(psL0, fT_bias[:, :], z1_lo[:, :], start=False, stop=True).then_inc(y0_ps, 1)

            def gate_sum(t):
                pe.wait_ge(gate_fold_ok, t + 1)
                nc.tensor.matmul(psLogit, ones[:, :], gate_fold[:, :, :], start=True, stop=True).then_inc(logit_ps, 1)

            def up(t, par, s):
                k = NS * t + s
                if not isinstance(t, int) or t == 0:
                    wait_weight_lo(pe, 2 * s)
                if s == 0:
                    pe.wait_ge(x1_hi_ok, t + 1)
                for c in range(CH):
                    n = CH * k + c
                    if not isinstance(n, int) or n >= UP:
                        pe.wait_ge(h_ok, n - UP + 1)
                    product_hi(up_bank(s, c), W1_hi[:, s, c, :], W1_lo[:, s, c, :], span(x1_hi[:, par, :], s), True)
                    if s == 0 and c == 0:
                        pe.wait_ge(x1_lo_ok, t + 1)
                    product_lo(up_bank(s, c), W1_hi[:, s, c, :], span(x1_lo[:, par, :], s), True).then_inc(up_ps, 1)

            def down(t, par, s):
                hf = half(par, s)
                if not isinstance(t, int):
                    wait_weight_lo(pe, 2 * s + 1)
                for c in range(CH):
                    if s == 0:
                        pe.wait_ge(shared_lo_ok, CH * t + c + 1)
                    elif c == 0:
                        pe.wait_ge(lo_ok, NB * (E * t + s))
                    last = product3(span(psY, s), W2_hi[:, s, c, :], W2_lo[:, s, c, :],
                                    span(hs_hi[:, hf, c, :], s), span(hs_lo[:, hf, c, :], s),
                                    s == 0 and c == 0, s == NS - 1 and c == CH - 1)
                if s == NS - 1:
                    last.then_inc(down_ok, 1)

            def down_halves(t, par, s):
                hf = half(par, s)
                steps = [(c, g) for c in range(CH) for g in range(2)]
                if s == NS - 1:
                    steps.sort(key=lambda step: step[1])
                for c, g in steps:
                    if s == 0 and g == 0:
                        if c == 0:
                            pe.wait_ge(logit_read, t + 1)
                        pe.wait_ge(shared_lo_ok, CH * t + c + 1)
                    elif s > 0 and c == 0:
                        pe.wait_ge(lo_ok, NB * (E * t + s - 1) + NB // 2 * (g + 1))
                    cols = slice(g * HALF, (g + 1) * HALF)
                    last = product3(span(psY_half[g], s), W2_hi[:, s, c, :], W2_lo[:, s, c, :],
                                    span(hs_hi[:, hf, c, cols], s), span(hs_lo[:, hf, c, cols], s),
                                    s == 0 and c == 0, s == NS - 1 and c == CH - 1)
                    if s == NS - 1 and c == CH - 1:
                        last.then_inc(down_ok, 1)

            def tile(t, par, last=False):
                down_ = down_halves if last else down
                if not last:
                    xT(t + 1, 1 - par)
                down_(t, par, 0)
                up(t, par, 2)
                if not last:
                    low_rank_in(t + 1)
                    transpose_F(t + 1, 1 - par)
                down_(t, par, 1)
                up(t, par, 3)
                if not last:
                    layer0(t + 1)
                down_(t, par, 2)
                up(t, par, 4)
                down_(t, par, 3)
                if not last:
                    up(t + 1, 1 - par, 0)
                    gate_sum(t + 1)
                down_(t, par, 4)
                if not last:
                    up(t + 1, 1 - par, 1)
                if last:
                    for g in range(2):
                        pe.wait_ge(outT_ok, NSEG * (t + g + 1))
                        for b in range(NB // 2):
                            at = g * HALF + b * L
                            tr = nc.tensor.transpose(psOut_half[g][:, b * D:(b + 1) * D], outT[:, at:at + L],
                                                     ident[:, :])
                        tr.then_inc(out_ps, 1)
                    return
                pe.wait_ge(outT_ok, NSEG * (t + 1))
                for b in range(NB):
                    tr = nc.tensor.transpose(psOut[:, b * D:(b + 1) * D], outT[:, b * L:(b + 1) * L], ident[:, :])
                tr.then_inc(out_ps, 1)

            pe.wait_ge(ones_ok, 1)
            keep_busy(7)
            pe.wait_ge(ident_ok, 1)
            xT(0, 0)
            keep_busy(2)
            pe.wait_ge(W_in, 16)
            nc.tensor.transpose(psWT, W_raw[:, :], ident[:, :]).then_inc(WT_ps, 1)
            pe.wait_ge(F_in[0], 32)
            transpose_F(0, 0)
            low_rank_in(0)
            pe.wait_ge(cond_in, 16)
            nc.tensor.transpose(psCondT, cond_raw[:, :], ident[0:B, 0:B]).then_inc(condT_ps, 1)
            pe.wait_ge(WT_lo_ok, 1)
            pe.wait_ge(z1_rows_ok, 1)
            layer0(0)
            keep_busy(11)
            up(0, 0, 0)
            pe.wait_ge(bias_in, 16 * 3)
            pe.wait_ge(silu_ok, 1)
            nc.tensor.transpose(psEb2T, eb2_raw[:, :], ident[0:E, 0:E]).then_inc(eb2T_ps, 1)
            pe.wait_ge(fT_lo_ok, 2)
            pe.wait_ge(mod_terms_ok, 1)
            nc.tensor.matmul(psMod, ones[:, :], mod_terms[:, :, :], start=True, stop=True).then_inc(mod_ps, 1)
            gate_sum(0)
            up(0, 0, 1)
            pe.wait_ge(mod_read, 1)
            pe.wait_ge(eb2T_read, 3)
            keep_busy(7, psOut[:, 0:128])
            with pe.Fori(0, NT - 3, 2) as t:
                tile(t, 0)
                tile(t + 1, 1)
            tile(NT - 2, 0)
            tile(NT - 1, 1, last=True)

        @block.vector
        def _(dve):
            n_setup = 0

            def chained(ins):
                nonlocal n_setup
                n_setup += 1
                ins.then_inc(setup_step, 1)
                dve.wait_ge(setup_step, n_setup)

            def F_split(t, par):
                dve.wait_ge(F_in[par], arrivals(t, par, 32))
                raw = F_raw[:, par, :, :].rearrange("i c r -> i (c r)")
                nc.vector.tensor_copy(F_hi[:, :], raw).then_inc(F_hi_ok, 1)
                dve.wait_ge(F_hi_ok, t + 1)
                nc.vector.tensor_tensor(F_lo[:, :], raw, f32(F_hi[:, :]), ALU.subtract
                                        ).then_inc(F_lo_ok, 1)

            def z1_mask(t):
                dve.wait_ge(z_ps, t + 1)
                src = psZ_first if isinstance(t, int) and t == 0 else psZ
                per_batch = "p (b l) -> p b l"
                nc.vector.tensor_tensor(z1[:, :].rearrange(per_batch, l=L), src.rearrange(per_batch, l=L),
                                        zmask[:, :].unsqueeze(2).to_broadcast([2 * ZR, NB, L]), ALU.mult
                                        ).then_inc(z1_ok, 1)

            def fT_low(t, par):
                dve.wait_ge(fT_hi_ok, t + 1)
                lo_rows = slice(BIAS_LO, BIAS_LO + NB)
                nc.vector.tensor_tensor(fT_bias[lo_rows, :], cond_rows[lo_rows, par, :], f32(fT_bias[lo_rows, :]),
                                        ALU.subtract).then_inc(fT_lo_ok, 1)
                nc.vector.tensor_tensor(fT[ZR:2 * ZR, :], psFT[ZR:2 * ZR, :], f32(fT[ZR:2 * ZR, :]), ALU.subtract
                                        ).then_inc(fT_lo_ok, 1)

            def residual0(t, par):
                dve.wait_ge(g0_ok, t + 1)
                xs = x1[:, par, :]
                nc.vector.tensor_tensor(xs, xs, g0[:, :], ALU.add).then_inc(x1_ok, 1)
                dve.wait_ge(x1_ok, t + 1)
                nc.vector.tensor_copy(x1_hi[:, par, :], xs).then_inc(x1_hi_ok, 1)
                dve.wait_ge(x1_hi_ok, t + 1)
                nc.vector.tensor_tensor(x1_lo[:, par, :], xs, f32(x1_hi[:, par, :]), ALU.subtract
                                        ).then_inc(x1_lo_ok, 1)

            def gate_in(t, par):
                x1v = x1[:, par, :].rearrange("p (b l) -> p b l", l=L)
                for i, (at, _, n) in enumerate(SEGS):
                    nc.vector.tensor_reduce(segsum[:, i, :], x1v[:, :, at:at + n], AX.X, ALU.add
                                            ).then_inc(segsum_ok, 1)
                dve.wait_ge(segsum_ok, NSEG * t + NSEG)
                nc.vector.tensor_tensor(gate_terms[:, :, :, :],
                                        segsum[:, :, :].unsqueeze(3).to_broadcast([128, NSEG, NB, E]),
                                        gw[:, :, :].unsqueeze(2).to_broadcast([128, NSEG, NB, E]),
                                        ALU.mult).then_inc(gate_terms_ok, 1)
                dve.wait_ge(gate_terms_ok, t + 1)
                nc.vector.tensor_reduce(gate_fold[:, :, :], gate_terms[:, :, :, :].rearrange("p s b e -> p b e s"),
                                        AX.X, ALU.add).then_inc(gate_fold_ok, 1)

            def linked(ins, t, n):
                ins.then_inc(gate_step, 1)
                dve.wait_ge(gate_step, GATE_LINKS * t + n)

            def gate_logits(t):
                dve.wait_ge(logit_ps, t + 1)
                nc.vector.tensor_tensor(logit[:, :, :], psLogit, gate_mul[:, bass.ds(t * NB, NB), :],
                                        ALU.mult).then_inc(logit_read, 1)
                dve.wait_ge(logit_read, t + 1)
                linked(nc.vector.tensor_tensor(logit[:, :, :], logit[:, :, :], gate_add[:, bass.ds(t * NB, NB), :],
                                               ALU.add), t, 1)
                linked(nc.vector.tensor_reduce(top[:, :], logit[:, :, :], AX.X, ALU.max), t, 2)
                nc.vector.tensor_tensor(logit_x[:, :, :], logit[:, :, :],
                                        top[:, :].unsqueeze(2).to_broadcast([128, NB, E]),
                                        ALU.subtract).then_inc(logit_x_ok, 1)
                logit_e = logit[:, :, :].unsqueeze(3).to_broadcast([128, NB, E, E])
                logit_j = logit[:, :, :].unsqueeze(2).to_broadcast([128, NB, E, E])
                linked(nc.vector.tensor_tensor(equal[:, :, :, :], logit_j, logit_e, ALU.is_equal), t, 3)
                nc.vector.tensor_tensor(greater[:, :, :, :], logit_j, logit_e, ALU.is_gt)
                linked(nc.vector.tensor_tensor(equal[:, :, :, :], equal[:, :, :, :], before[:, :, :, :],
                                               ALU.mult), t, 4)
                linked(nc.vector.tensor_tensor(greater[:, :, :, :], greater[:, :, :, :], equal[:, :, :, :],
                                               ALU.add), t, 5)

            def gate_weights(t):
                dve.wait_ge(tanh_g_ok, t + 1)
                nc.vector.tensor_reduce(rank[:, :, :], greater[:, :, :, :], AX.X, ALU.add)
                linked(nc.vector.tensor_scalar(denom[:, :, :], tanh_g[:, :, :], -1.0, 1.0, ALU.mult, ALU.add), t, 6)
                nc.vector.tensor_scalar(numer[:, :, :], tanh_g[:, :, :], 1.0, None, ALU.add)
                linked(nc.vector.reciprocal(denom[:, :, :], denom[:, :, :]), t, 7)
                nc.vector.tensor_scalar(chosen[:, :, :], rank[:, :, :], 1.5, None, ALU.is_lt)
                linked(nc.vector.tensor_tensor(expd[:, :, :], numer[:, :, :], denom[:, :, :], ALU.mult), t, 8)
                nc.vector.tensor_reduce(sum_all[:, :], expd[:, :, :], AX.X, ALU.add)
                linked(nc.vector.tensor_tensor(exp_top[:, :, :], expd[:, :, :], chosen[:, :, :], ALU.mult), t, 9)
                linked(nc.vector.tensor_reduce(sum_top[:, :], exp_top[:, :, :], AX.X, ALU.add), t, 10)
                linked(nc.vector.scalar_tensor_tensor(sum_top[:, :], sum_all[:, :], 1e-8, sum_top[:, :],
                                                      ALU.mult, ALU.add), t, 11)
                linked(nc.vector.reciprocal(sum_top[:, :], sum_top[:, :]), t, 12)
                nc.vector.tensor_tensor(w_be[:, :, :], exp_top[:, :, :],
                                        sum_top[:, :].unsqueeze(2).to_broadcast([128, NB, E]),
                                        ALU.mult).then_inc(w_ok, 1)

            def output_biases(t):
                for i in range(NSEG):
                    ins = nc.vector.tensor_tensor(bias_terms[:, i, :, :], w_be[:, :, :],
                                                  eb2T[:, i, :].unsqueeze(1).to_broadcast([128, NB, E]), ALU.mult)
                linked(ins, t, 13)
                linked(nc.vector.tensor_reduce(bias2[:, :, :], bias_terms[:, :, :, :], AX.X, ALU.add), t, 14)
                nc.vector.tensor_scalar(bias2[:, :, :], bias2[:, :, :], sb2_col[:, 0:1], None, ALU.add
                                        ).then_inc(bias2_ok, 1)

            def split(t, par, s, last=False):
                hf = half(par, s)
                a, z = SPAN[s]
                dve.wait_ge(h_ok, CH * (NS * t + s + 1))
                if s == 1:
                    dve.wait_ge(w_ok, t + 1)
                own = NB if s < E else int(last)
                for b in range(own):
                    c = slice(b * L + a, b * L + z)
                    nc.vector.tensor_scalar(hs_hi[:, hf, :, c], h[:, hf, :, c], w_be[:, b, s - 1:s], None,
                                            ALU.mult).then_inc(hi_ok, 1)
                for b in range(NB):
                    c = slice(b * L + a, b * L + z)
                    if b < own:
                        dve.wait_ge(hi_ok, NB * ((E - 1) * t + s - 1) + b + 1)
                    else:
                        dve.wait_ge(hi4_ok, NB * t + b + 1 - int(last))
                    nc.vector.scalar_tensor_tensor(hs_lo[:, hf, :, c], h[:, hf, :, c], w_be[:, b, s - 1:s],
                                                   f32(hs_hi[:, hf, :, c]), ALU.mult, ALU.subtract
                                                   ).then_inc(lo_ok, 1)

            def tile(t, par, last=False, F_next=True):
                split(t, par, 1)
                if not last:
                    z1_mask(t + 1)
                output_biases(t)
                if not last:
                    fT_low(t + 1, 1 - par)
                split(t, par, 2)
                split(t, par, 3)
                if not last:
                    residual0(t + 1, 1 - par)
                    gate_in(t + 1, 1 - par)
                split(t, par, 4, last)
                dve.wait_ge(x1b_ok, NSEG * (t + 1))
                if not last:
                    gate_logits(t + 1)
                for g in range(2 if last else 1):
                    dve.wait_ge(down_ok, t + g + 1)
                    cols = slice(g * HALF, (g + 1) * HALF) if last else slice(0, TOK)
                    summed = psY_half[g] if last else psY
                    dst_v, sum_v, x1_v = (ap.rearrange("p (b l) -> p b l", l=L)
                                          for ap in (outT[:, cols], summed, x1[:, par, cols]))
                    for at, dst, n in SEGS:
                        nc.vector.tensor_tensor(dst_v[:, :, dst:dst + n], sum_v[:, :, at:at + n],
                                                x1_v[:, :, at:at + n], ALU.add).then_inc(outT_ok, 1)
                if not last:
                    gate_weights(t + 1)
                if F_next:
                    F_split(t + 2, par)

            nc.vector.memset(cond_rows[BIAS_HI:128, :, :], 0.0).then_inc(rows_zero_ok, 1)
            dve.wait_ge(batch_rows_ok, 1)
            nc.vector.tensor_copy(z1_lo[BIAS_HI:128, :].rearrange("p (b l) -> p b l", l=L),
                                  batch_rows[BIAS_HI:128, :].unsqueeze(2).to_broadcast([128 - BIAS_HI, NB, L])
                                  ).then_inc(z1_rows_ok, 1)
            F_split(0, 0)
            dve.wait_ge(xT_hi_ok, 1)
            nc.vector.tensor_tensor(xT_lo[:, :], psL0, f32(xT_hi[:, :]), ALU.subtract).then_inc(xT_lo_ok, 1)
            dve.wait_ge(WT_hi_ok, 1)
            nc.vector.tensor_tensor(WT_lo[:, :], psWT, f32(WT_hi[:, :]), ALU.subtract).then_inc(WT_lo_ok, 1)
            dve.wait_ge(zmask_ok, 1)
            z1_mask(0)
            fT_low(0, 0)
            make_weight_hi(dve, 1)
            dve.wait_ge(z1_hi_ok, 1)
            nc.vector.tensor_tensor(z1_lo[0:ZR, :], z1[0:ZR, :], f32(z1_hi[0:ZR, :]), ALU.subtract
                                    ).then_inc(z1_lo_ok, 1)
            make_weight_lo(dve, 0)
            make_weight_lo(dve, 2)
            make_weight_hi(dve, 4)
            residual0(0, 0)
            dve.wait_ge(tanh_c_ok, 1)
            nc.vector.scalar_tensor_tensor(silu2[:, :], tanh_c[:, :], 1.0, psCondT, ALU.add, ALU.mult
                                           ).then_inc(silu_ok, 1)
            dve.wait_ge(gate_loads_in, 16 * 3)
            chained(nc.vector.tensor_scalar(tw[:, :], time_w_raw[:, :], 0.5, None, ALU.mult))
            dve.wait_ge(silu_ok, 1)
            nc.vector.tensor_tensor(mod_terms[:, :, :], silu2[:, :].unsqueeze(2).to_broadcast([128, B, 2 * E]),
                                    tw[:, :].unsqueeze(1).to_broadcast([128, B, 2 * E]), ALU.mult
                                    ).then_inc(mod_terms_ok, 1)
            inv = 1.0 / (HEAD + PROP)
            chained(nc.vector.tensor_scalar(gw_full[:, :], gate_raw[:, 0, :], 1.0 / L, None, ALU.mult))
            chained(nc.vector.scalar_tensor_tensor(gw[:, 0, :], gate_raw[:, 1, :], inv, gw_full[:, :],
                                                   ALU.mult, ALU.add))
            nc.vector.scalar_tensor_tensor(gw[:, 2, :], gate_raw[:, 2, :], inv, gw_full[:, :], ALU.mult, ALU.add)
            chained(nc.vector.scalar_tensor_tensor(gw[:, 1, :], gate_raw[:, 2, :], inv, gw[:, 0, :],
                                                   ALU.mult, ALU.add))
            gate_in(0, 0)
            dve.wait_ge(eb2T_ps, 1)
            for i in range(NSEG):
                nc.vector.tensor_copy(eb2T[:, i, :], psEb2T).then_inc(eb2T_read, 1)
            dve.wait_ge(eb2T_read, NSEG)
            nc.vector.memset(eb2T[:, 2, 1:2], 0.0)
            chained(nc.vector.memset(eb2T[:, 0, 2:3], 0.0))
            dve.wait_ge(mod_ps, 1)
            dve.wait_ge(bias_in, 16 * 3)
            nc.vector.tensor_tensor(mod[:, :, :], psMod, time_b_row[:, :].unsqueeze(1).to_broadcast([128, B, 2 * E]),
                                    ALU.add).then_inc(mod_read, 1)
            dve.wait_ge(mod_read, 1)
            chained(nc.vector.tensor_scalar(gate_mul[:, :, :], mod[:, :, 0:E], 1.0, None, ALU.add))
            chained(nc.vector.tensor_tensor(gate_add[:, :, :], gate_mul[:, :, :],
                                            gate_b_row[:, :].unsqueeze(1).to_broadcast([128, B, E]), ALU.mult))
            chained(nc.vector.tensor_tensor(gate_add[:, :, :], gate_add[:, :, :], mod[:, :, E:2 * E], ALU.add))
            dve.wait_ge(before_ok, 1)
            gate_logits(0)
            make_weight_lo(dve, 6)
            F_split(1, 1)
            gate_weights(0)
            with dve.Fori(0, NT - 3, 2) as t:
                tile(t, 0)
                tile(t + 1, 1)
            tile(NT - 2, 0, F_next=False)
            tile(NT - 1, 1, last=True, F_next=False)


_INS = ["x", "fside_Bx1x1024x16_0", "cond_1024", "L0_cond_W", "L0_cond_fc_bias", "L1_cond_gate_w", "L1_cond_gate_b",
        "L1_cond_time_w", "L1_cond_time_b", "L1_cond_ew1", "L1_cond_eb1", "L1_cond_ew2", "L1_cond_eb2",
        "L1_cond_sw1", "L1_cond_sb1", "L1_cond_sw2", "L1_cond_sb2"]


def kernel(**inputs):
    import numpy as np
    import concourse.bacc as bacc
    from concourse.bass_utils import run_bass_kernel_spmd

    nc = bacc.Bacc("TRN2", target_bir_lowering=False, num_devices=1)
    arrays, args = {}, []
    for name in _INS:
        a = np.ascontiguousarray(inputs[name])
        arrays[f"in_{name}"] = a
        args.append(nc.dram_tensor(f"in_{name}", a.shape, mybir.dt.from_np(a.dtype), kind="ExternalInput").ap())
    shape = arrays["in_x"].shape
    args.append(nc.dram_tensor("out_0", shape, F32, kind="ExternalOutput").ap())
    build(nc, *args)
    r = run_bass_kernel_spmd(nc, [arrays], core_ids=[0])
    return r.results[0]["out_0"]
```
